# Optimizing a Trainium2 kernel written in Bass

```python
import numpy as np
import jax
import jax.numpy as jnp

def _softmax(x, axis=-1):
    return jax.nn.softmax(x, axis=axis)

def _gelu(x):
    return jax.nn.gelu(x, approximate=True)

def _silu(x):
    return jax.nn.silu(x)

def _sigmoid(x):
    return jax.nn.sigmoid(x)

def _layernorm(x, axis=-1, eps=1e-05):
    m = jnp.mean(x, axis=axis, keepdims=True)
    v = jnp.var(x, axis=axis, keepdims=True)
    return (x - m) / jnp.sqrt(v + eps)

def _scatter_add(tgt, idx, src, axis=0):
    return tgt.at[idx].add(src)

def _segment_sum(src, seg, n):
    return jax.ops.segment_sum(src, seg, n)
kernel_name = 'mk_adj_preln_d2_adj_r2_4e5a16'

def setup_inputs(seed: int=0):
    np.random.seed(seed)
    _w = jnp.asarray

    def _rec_inputs():
        import jax
        import jax.numpy as jnp
        _gk = jax.random.key(seed)
        x = -0.000929 + 1 * jax.random.normal(jax.random.fold_in(_gk, 1), (8192, 128), jnp.float32)
        _w = (1.0 + jnp.arange(8192, dtype=jnp.float32)) ** (-0.5)
        _w = _w / _w.mean()
        _pij = jnp.clip(0.000488281 * _w[:, None] * _w[None, :], 0.0, 1.0)
        _a = jax.random.uniform(jax.random.fold_in(_gk, 2), (8192, 8192)) < _pij
        _a = jnp.logical_or(_a, jnp.eye(8192, dtype=bool))
        _af = _a.astype(jnp.float32)
        _af = _af * jax.random.uniform(jax.random.fold_in(_gk, 3), (8192, 8192), jnp.float32, 0.05, 1)
        adj = _af
        return (x, adj)
    x, adj = _rec_inputs()

    def _L0_gnn_setup():
        import jax, jax.numpy as jnp
        import numpy as np
        CUTOFF = 0.5
        key = jax.random.key(seed)
        k_z, k_d, k_w, k_mu, k_sg = jax.random.split(key, 5)
        N, D_IN, D_OUT = (4096, 128, 128)
        z = jax.random.normal(k_z, (N, D_IN), dtype=jnp.float32)
        dist_matrix = jax.random.uniform(k_d, (N, N), dtype=jnp.float32)
        W = jax.random.normal(k_w, (D_IN, D_OUT), dtype=jnp.float32)
        B = jnp.zeros((D_OUT,), dtype=jnp.float32)
        mu = jax.random.normal(k_mu, (1,), dtype=jnp.float32)
        sigma = jax.random.normal(k_sg, (1,), dtype=jnp.float32)
        return {'z': z, 'dist_matrix': dist_matrix, 'W': W, 'B': B, 'mu': mu, 'sigma': sigma}
    _L0_gnn_all = _L0_gnn_setup()
    _L0_gnn_in = {k: v for k, v in _L0_gnn_all.items() if k in ('W', 'B', 'mu', 'sigma')}
    del _L0_gnn_all

    def _L1_gnn_setup():
        import jax, jax.numpy as jnp
        import numpy as np
        N = 4096
        C_IN = 128
        C_OUT = 128
        key = jax.random.key(seed)
        k1, k2, k3, k4 = jax.random.split(key, 4)
        x = jax.random.normal(k1, (N, C_IN), dtype=jnp.float32)
        adj = jax.random.uniform(k2, (N, N), dtype=jnp.float32)
        mask = jax.random.uniform(k3, (N, N), dtype=jnp.float32)
        W = jax.random.normal(k4, (C_OUT, C_IN), dtype=jnp.float32) * (1.0 / np.sqrt(C_IN))
        return {'x': x, 'adj': adj, 'mask': mask, 'W': W}
    _L1_gnn_all = _L1_gnn_setup()
    _L1_gnn_in = {k: v for k, v in _L1_gnn_all.items() if k in ('W',)}
    del _L1_gnn_all
    return {'x': x, 'adj': adj, 'L0_gnn_W': _L0_gnn_in['W'], 'L0_gnn_B': _L0_gnn_in['B'], 'L0_gnn_mu': _L0_gnn_in['mu'], 'L0_gnn_sigma': _L0_gnn_in['sigma'], 'L1_gnn_W': _L1_gnn_in['W']}

def reference(x, adj, L0_gnn_W, L0_gnn_B, L0_gnn_mu, L0_gnn_sigma, L1_gnn_W):
    import jax
    import jax.numpy as jnp

    def _L0_gnn_ref(z, dist_matrix, W, B, mu, sigma):
        import jax, jax.numpy as jnp
        import numpy as np
        CUTOFF = 0.5
        N = dist_matrix.shape[0]
        h = z @ W + B
        mask = (dist_matrix < CUTOFF) & ~jnp.eye(N, dtype=bool)
        r = jnp.where(mask, dist_matrix, 1.0)
        sens = jnp.exp(-(1.0 / r - 1.0 / mu[0]) ** 2 / (2.0 * sigma[0] ** 2))
        S = jnp.where(mask, sens, 0.0)
        return S @ h

    def _L1_gnn_ref(x, adj, mask, W):
        import jax, jax.numpy as jnp
        import numpy as np
        N = 4096
        C_IN = 128
        C_OUT = 128
        n = adj.shape[0]
        adj_eff = adj * mask + jnp.eye(n, dtype=adj.dtype)
        h = jnp.einsum('nc,oc->no', x, W)
        return jnp.matmul(adj_eff, h)
    h = jnp.maximum(_layernorm(x, axis=-1), 0.0)
    x = x + _L0_gnn_ref(h, adj, L0_gnn_W, L0_gnn_B, L0_gnn_mu, L0_gnn_sigma)
    h = jnp.maximum(_layernorm(x, axis=-1), 0.0)
    x = x + _L1_gnn_ref(h, adj, adj, L1_gnn_W)
    return x

_drawn_inputs = setup_inputs


def setup_inputs(seed=0):
    import zlib

    import numpy as np

    out = dict(_drawn_inputs(seed))
    spreads = {'L0_gnn_B': (0.0, 0.8)}
    factors = {'L0_gnn_W': 7.581}
    for name, (base, spread) in spreads.items():
        noise = np.random.default_rng([zlib.crc32(name.encode()), seed]).standard_normal(out[name].shape)
        drawn = base * np.exp(spread * noise) if base else spread * noise
        out[name] = jnp.asarray(drawn.astype(out[name].dtype))
    for name, factor in factors.items():
        out[name] = (out[name] * factor).astype(out[name].dtype)
    return out
```

```python
from contextlib import ExitStack

import concourse.bass as bass
from concourse import mybir

ALU = mybir.AluOpType
ACT = mybir.ActivationFunctionType
F32 = mybir.dt.float32

P = 128
D = 128
N = 8192
CHUNK = 512
NC = N // CHUNK
G = CHUNK // P
TILE = G * CHUNK
GROUP = 4
NG = NC // GROUP
A_RING = 4
S_RING = 8
Q_RING = 2
DIAG = CHUNK + P
LN_EPS = 1e-5
CUTOFF = 0.5
TINY = 2.0 ** -60


def order_of(s):
    with_l2, without = iter(range(GROUP * s)), iter(range(GROUP * s, NC))
    n = GROUP * s
    return [next(with_l2) if (i + 1) * n // NC > i * n // NC else next(without) for i in range(NC)]


ORDER = [order_of(s) for s in range(NG)]
L2_BASE = [sum(GROUP * GROUP * r for r in range(s)) for s in range(NG + 1)]
L2_RANK = [[sum(J < GROUP * s for J in ORDER[s][:i]) for i in range(NC + 1)] for s in range(NG)]
PH1 = NC * NC
PH2_N = [NC - GROUP * s for s in range(NG)]
PH2_BASE = [GROUP * sum(PH2_N[:s]) for s in range(NG)]


def l2_before(s, c, i):
    return L2_BASE[s] + (c - GROUP * s) * (GROUP * s) + L2_RANK[s][i]


def l2_before_back(s, c, i, back):
    if i >= back:
        return l2_before(s, c, i - back)
    if isinstance(c, int):
        return l2_before((c - 1) // GROUP, c - 1, i - back + NC) if c else 0
    return l2_before(s, c - 1, i - back + NC)


def ph2_before(s, c, k):
    return PH2_BASE[s] + (c - GROUP * s) * PH2_N[s] + k


def phase1_chunks(eng, body):
    for s in range(NG):
        first = max(1, GROUP * s)
        body(s, first)
        with eng.Fori(first + 1, GROUP * (s + 1)) as c:
            body(s, c)


def phase2_pairs(eng, body, pair0_apart=True, last_apart=False):
    for s in range(NG):
        lo, hi = GROUP * s, GROUP * (s + 1)
        if (s == 0 and pair0_apart) or (s == NG - 1 and last_apart):
            for c in range(lo, hi, 2):
                body(s, c)
        else:
            with eng.Fori(lo // 2, hi // 2) as half:
                body(s, half * 2)


def gnn_program(nc, xT, adjT, W0, B0, mu, sigma, W1T, outT):
    with ExitStack() as ctx:
        def sb(name, shape):
            return ctx.enter_context(nc.sbuf_tensor(name, shape, F32))

        def bank(name):
            return ctx.enter_context(nc.psum_tensor(name, [P, CHUNK], F32))

        def sem(name):
            return ctx.enter_context(nc.semaphore(name))

        acc_dram = nc.dram_tensor("acc_dram", [D, N], F32).ap()

        a_ring = sb("a_ring", [P, A_RING * TILE + CHUNK])
        s_ring = sb("s_ring", [P, S_RING * TILE + CHUNK])
        q_ring = sb("q_ring", [P, Q_RING * TILE])
        h1 = sb("h1", [P, NC * G, D])
        h2 = sb("h2", [P, NC * G, D])
        x_buf = [sb(f"x_buf{n}", [D, CHUNK]) for n in range(2)]
        centred_buf = [sb(f"centred_buf{n}", [D, CHUNK]) for n in range(3)]
        square_buf = [sb(f"square_buf{n}", [D, CHUNK]) for n in range(2)]
        rstd_buf = [sb(f"rstd_buf{n}", [D, CHUNK]) for n in range(2)]
        normed_buf = [sb(f"normed_buf{n}", [D, CHUNK]) for n in range(2)]
        acc_buf = square_buf[1]
        acc_in = rstd_buf
        out_buf = normed_buf
        bias_rows = sb("bias_rows", [P, D])
        w0 = sb("w0", [D, D])
        w1 = sb("w1", [D, D])
        mean_of = sb("mean_of", [D, D])
        eye_strip = sb("eye_strip", [P, (2 * GROUP - 1) * P])
        small = sb("small", [P, 16])
        mu_c, sigma_c, inv_mu, neg_2c, var2, inv_var2, neg_k, c_sq, exp_bias, tiny_c, eps_c = (
            small[:, n:n + 1] for n in range(11))

        p_l1 = bank("p_l1")
        p_l2 = [bank("p_l2a"), bank("p_l2b")]
        p_stat = [bank("p_stat0"), bank("p_stat1"), bank("p_stat2"), p_l2[1]]
        p_proj = [bank("p_proj0"), bank("p_proj1")]

        a_loaded = [sem(f"a_loaded{n}") for n in range(A_RING)]
        x_loaded = [sem("x_loaded0"), sem("x_loaded1")]
        weights_loaded = sem("weights_loaded")
        params_loaded = sem("params_loaded")
        param_step = sem("param_step")
        strip_zeroed = sem("strip_zeroed")
        strip_ready = sem("strip_ready")
        diag_marked = sem("diag_marked")
        premasked = sem("premasked")
        ln_done = sem("ln_done")
        recip_done = sem("recip_done")
        squared = sem("squared")
        sens_done = sem("sens_done")
        s_used = sem("s_used")
        q_ready = sem("q_ready")
        q_used = sem("q_used")
        x1_added = sem("x1_added")
        acc_added = sem("acc_added")
        acc_stored = sem("acc_stored")
        mean_done = sem("mean_done")
        centred = sem("centred")
        dev_squared = sem("dev_squared")
        var_done = sem("var_done")
        log_var_done = sem("log_var_done")
        rstd_done = sem("rstd_done")
        normed = sem("normed")
        projected = sem("projected")
        h_ready = sem("h_ready")
        sq2_ready = sem("sq2_ready")
        eye_added = sem("eye_added")
        final_done = sem("final_done")
        acc_loaded = [sem("acc_loaded0"), sem("acc_loaded1")]
        out_stored = [sem("out_stored0"), sem("out_stored1")]

        def a_tile(slot):
            return a_ring[:, slot * TILE:(slot + 1) * TILE]

        def s_tile(slot):
            return s_ring[:, slot * TILE:(slot + 1) * TILE]

        def q_tile(slot):
            return q_ring[:, slot * TILE:(slot + 1) * TILE]

        def diagonal(ring, slot):
            v = ring[:, slot * TILE:slot * TILE + G * DIAG]
            return v.rearrange("p (g n) -> p g n", g=G)[:, :, 0:P]

        def eye_if_diagonal(J, c, s):
            first = c * P + (GROUP - 1 - J) * P
            return eye_strip[:, bass.ds(first, P)].unsqueeze(1).to_broadcast([P, G, P])

        def adj_tile(c, J):
            return adjT[bass.ds(c * NC + J, 1), :, :].rearrange("t p n -> p (t n)")

        def columns(dram, c):
            return dram[:, bass.ds(c * CHUNK, CHUNK)]

        block = ctx.enter_context(nc.Block())

        @block.sync
        def _(sp):
            def load_tile(s, c, i):
                J, t = ORDER[s][i], c * NC + i
                if not (isinstance(c, int) and t < A_RING):
                    n = l2_before_back(s, c, i, A_RING - 1)
                    if not isinstance(n, int):
                        sp.compute_val(n)
                    sp.wait_ge(premasked, t - A_RING + 1)
                    if not (isinstance(n, int) and n == 0):
                        sp.wait_ge(q_ready, n)
                sp.dma_start(a_tile(i % A_RING), adj_tile(c, J)).then_inc(a_loaded[i % A_RING], 16)

            def load_x(n):
                if n >= 2:
                    sp.wait_ge(centred, n - 1)
                sp.dma_start(x_buf[n % 2][:, :], columns(xT, n)).then_inc(x_loaded[n % 2], 16)

            load_x(0)
            sp.dma_start(mu_c, mu.partition_broadcast(P)).then_inc(params_loaded, 16)
            sp.dma_start(sigma_c, sigma.partition_broadcast(P)).then_inc(params_loaded, 16)
            load_tile(0, 0, 0)
            sp.dma_start(w0[:, :], W0).then_inc(weights_loaded, 16)
            sp.dma_start(w1[:, :], W1T).then_inc(weights_loaded, 16)
            sp.dma_start(bias_rows[:, :], B0.partition_broadcast(P)).then_inc(weights_loaded, 16)
            load_x(1)
            for i in range(1, NC):
                load_tile(0, 0, i)
                if 2 <= i:
                    load_x(i)

            def chunk(s, c):
                for i in range(NC):
                    load_tile(s, c, i)
                    if i == 3:
                        sp.wait_ge(centred, c + NC - 1)
                        sp.dma_start(x_buf[0][:, :], columns(xT, c - 1)).then_inc(x_loaded[0], 16)
                    if i == 9:
                        sp.wait_ge(acc_added, c)
                        sp.dma_start(columns(acc_dram, c - 1), acc_buf[:, :]).then_inc(acc_stored, 16)

            phase1_chunks(sp, chunk)
            sp.wait_ge(centred, 2 * NC - 1)
            sp.dma_start(x_buf[0][:, :], columns(xT, NC - 1)).then_inc(x_loaded[0], 16)

            def load_tile2(s, c, k):
                n = ph2_before(s, c, k)
                if isinstance(n, int) and n < A_RING:
                    sp.wait_ge(premasked, PH1 + n - A_RING + 1)
                    sp.wait_ge(q_ready, l2_before(NG - 1, NC - 1, NC + n - A_RING + 1))
                else:
                    sp.wait_ge(sq2_ready, n - A_RING + 1)
                sp.dma_start(a_tile(k % A_RING), adj_tile(c, GROUP * s + k)).then_inc(
                    a_loaded[k % A_RING], 16)

            def pair(s, c0):
                for c in (c0, c0 + 1):
                    for k in range(PH2_N[s]):
                        load_tile2(s, c, k)
                        if isinstance(c, int) and c == 0 and k == 9:
                            sp.wait_ge(acc_added, NC)
                            sp.dma_start(columns(acc_dram, NC - 1), acc_buf[:, :]).then_inc(
                                acc_stored, 16)

            phase2_pairs(sp, pair)

        @block.tensor
        def _(pe):
            def l1(s, c, i):
                J, t = ORDER[s][i], c * NC + i
                if isinstance(c, int) and c == 0:
                    pe.wait_ge(h_ready, J + 1)
                elif i == 0:
                    pe.wait_ge(x1_added, c)
                pe.wait_ge(sens_done, t + 1)
                for g in range(G):
                    last = pe.matmul(p_l1[:, :], h1[:, J * G + g, :],
                                     s_tile(i % S_RING)[:, g * CHUNK:(g + 1) * CHUNK],
                                     start=(i == 0 and g == 0), stop=(i == NC - 1 and g == G - 1))
                last.then_inc(s_used, 1)

            def l2(s, c, i):
                J, r = ORDER[s][i], L2_RANK[s][i]
                if r == 0:
                    pe.wait_ge(acc_added, c)
                pe.wait_ge(h_ready, NC + J + 1)
                pe.wait_ge(q_ready, l2_before(s, c, i) + 1)
                for g in range(G):
                    last = pe.matmul(p_l2[0][:, :], h2[:, J * G + g, :],
                                     q_tile(r % Q_RING)[:, g * CHUNK:(g + 1) * CHUNK],
                                     start=(r == 0 and g == 0),
                                     stop=(r == GROUP * s - 1 and g == G - 1))
                last.then_inc(q_used, 1)

            def mean(n, b):
                if b is None:
                    pe.wait_ge(rstd_done, n)
                elif n >= 4:
                    pe.wait_ge(rstd_done, n - 3)
                if b is not None:
                    pe.wait_ge(x_loaded[b], 16 * (n // 2 + 1))
                sb_ = 0 if b is None else n % 4
                b = b or 0
                pe.matmul(p_stat[sb_][:, :], mean_of[:, :], x_buf[b][:, :], start=True,
                          stop=True).then_inc(mean_done, 1)

            def variance(n, b, stat):
                pe.wait_ge(dev_squared, n + 1)
                pe.matmul(p_stat[stat][:, :], mean_of[:, :], square_buf[b][:, :], start=True,
                          stop=True).then_inc(var_done, 1)

            def project(n, b, w, apart):
                pe.wait_ge(normed, n + 1)
                if not (isinstance(n, int) and n < 2):
                    pe.wait_ge(h_ready, n - 1 if apart else n)
                for g in range(G):
                    last = pe.matmul(p_proj[b][:, g * P:(g + 1) * P],
                                     normed_buf[b][:, g * P:(g + 1) * P], w[:, :],
                                     start=True, stop=True)
                last.then_inc(projected, 1)

            pe.wait_ge(param_step, 2)
            mean(0, 0)
            for m in range(NC + 3):
                if m + 1 < NC:
                    mean(m + 1, (m + 1) % 2)
                if m >= 5:
                    l1(0, 0, m - 5)
                if m < NC:
                    variance(m, m % 2, m % 4)
                if m == 3:
                    pe.wait_ge(weights_loaded, 48)
                if m >= 3:
                    project(m - 3, (m - 3) % 2, w0, True)
            for i in (NC - 2, NC - 1):
                l1(0, 0, i)

            def chunk(s, c):
                for i in range(NC):
                    l1(s, c, i)
                    if i == 0:
                        mean(c + NC - 1, None)
                    if ORDER[s][i] < GROUP * s:
                        l2(s, c, i)
                    if i == 3:
                        variance(c + NC - 1, 0, 0)
                    if i == 6:
                        project(c + NC - 1, 0, w1, False)

            phase1_chunks(pe, chunk)

            def l2_rest(s, c, par, k):
                J, n = GROUP * s + k, ph2_before(s, c, k)
                if isinstance(c, int) and c == 0:
                    pe.wait_ge(h_ready, NC + J + 1)
                if k < GROUP:
                    pe.wait_ge(eye_added, c * GROUP + k + 1)
                else:
                    pe.wait_ge(sq2_ready, n + 1)
                slot = (par * PH2_N[s] + k) % S_RING
                for g in range(G):
                    last = pe.matmul(p_l2[1 - par][:, :], h2[:, J * G + g, :],
                                     s_tile(slot)[:, g * CHUNK:(g + 1) * CHUNK],
                                     start=(k == 0 and g == 0),
                                     stop=(k == PH2_N[s] - 1 and g == G - 1))
                last.then_inc(s_used, 1)

            def pair(s, c0):
                for par in range(2):
                    c = c0 + par
                    if isinstance(c, int) and c == 1:
                        pe.wait_ge(acc_added, NC)
                    if not (isinstance(c, int) and c < 2):
                        pe.wait_ge(final_done, c - 1)
                    for k in range(PH2_N[s]):
                        if isinstance(c, int) and c == 0 and k == 0:
                            pe.wait_ge(x1_added, NC)
                            mean(2 * NC - 1, None)
                        l2_rest(s, c, par, k)
                        if isinstance(c, int) and c == 0:
                            if k == 1:
                                variance(2 * NC - 1, 0, 0)
                            if k == 6:
                                project(2 * NC - 1, 0, w1, False)

            phase2_pairs(pe, pair)

        @block.vector
        def _(dve):
            steps = [0]

            def small_step(instruction):
                steps[0] += 1
                instruction.then_inc(param_step, 1)
                dve.wait_ge(param_step, steps[0])

            dve.memset(eye_strip[:, :], 0.0).then_inc(strip_zeroed, 1)
            small_step(dve.memset(tiny_c, TINY))
            small_step(dve.memset(mean_of[:, :], 1.0 / D))
            small_step(dve.memset(eps_c, LN_EPS))
            dve.wait_ge(params_loaded, 32)
            small_step(dve.reciprocal(inv_mu, mu_c))
            small_step(dve.tensor_scalar(neg_2c, inv_mu, -2.0, None, ALU.mult))
            small_step(dve.tensor_tensor(var2, sigma_c, sigma_c, ALU.mult))
            small_step(dve.tensor_scalar(var2, var2, 2.0, None, ALU.mult))
            small_step(dve.reciprocal(inv_var2, var2))
            small_step(dve.tensor_scalar(neg_k, inv_var2, -1.0, None, ALU.mult))
            small_step(dve.tensor_tensor(c_sq, inv_mu, inv_mu, ALU.mult))
            small_step(dve.tensor_tensor(exp_bias, c_sq, neg_k, ALU.mult))
            dve.wait_ge(strip_ready, 1)

            def premask(s, c, i):
                J, t = ORDER[s][i], c * NC + i
                dve.wait_ge(a_loaded[i % A_RING], 16 * (c * (NC // A_RING) + i // A_RING + 1))
                if GROUP * s <= J < GROUP * (s + 1):
                    d = diagonal(a_ring, i % A_RING)
                    dve.tensor_tensor(d, d, eye_if_diagonal(J, c, s), ALU.add).then_inc(diag_marked, 1)
                    dve.wait_ge(diag_marked, c * GROUP + J - GROUP * s + 1)
                if not (isinstance(c, int) and t < S_RING):
                    dve.wait_ge(s_used, t - S_RING + 1)
                dve.scalar_tensor_tensor(out=s_tile(i % S_RING), in0=a_tile(i % A_RING), scalar=CUTOFF,
                                         in1=a_tile(i % A_RING), op0=ALU.is_lt,
                                         op1=ALU.mult).then_inc(premasked, 1)

            def square(t, slot):
                dve.wait_ge(recip_done, t + 1)
                v = s_tile(slot)
                dve.scalar_tensor_tensor(out=v, in0=v, scalar=neg_2c, in1=v, op0=ALU.add,
                                         op1=ALU.mult).then_inc(squared, 1)

            def centre(n, b, cb, stat):
                if isinstance(n, int) and 3 <= n < NC:
                    dve.wait_ge(normed, n - 2)
                dve.wait_ge(mean_done, n + 1)
                dve.tensor_tensor(centred_buf[cb][:, :], x_buf[b][:, :], p_stat[stat][:, :],
                                  ALU.subtract).then_inc(centred, 1)

            def norm_relu(n, b, cb, apart):
                dve.wait_ge(rstd_done, n + 1)
                if not (isinstance(n, int) and n < 2):
                    dve.wait_ge(projected, n - 1 if apart else n)
                dve.scalar_tensor_tensor(out=normed_buf[b][:, :], in0=centred_buf[cb][:, :], scalar=0.0,
                                         in1=rstd_buf[b][:, :], op0=ALU.max,
                                         op1=ALU.mult).then_inc(normed, 1)

            def keep_h1(n):
                dve.wait_ge(projected, n + 1)
                if n == 0:
                    dve.wait_ge(weights_loaded, 48)
                dve.tensor_tensor(h1[:, n * G:(n + 1) * G, :],
                                  p_proj[n % 2][:, :].rearrange("p (g n) -> p g n", g=G),
                                  bias_rows[:, :].unsqueeze(1).to_broadcast([P, G, D]),
                                  ALU.add).then_inc(h_ready, 1)

            def keep_h2(c):
                dve.wait_ge(projected, c + NC + 1)
                dve.tensor_copy(h2[:, bass.ds(c * G, G), :],
                                p_proj[0][:, :].rearrange("p (g n) -> p g n", g=G)).then_inc(h_ready, 1)

            def add_x1(c):
                dve.wait_ge(s_used, (c + 1) * NC)
                dve.wait_ge(x_loaded[0], 16 * (c + NC // 2 + 1))
                dve.tensor_tensor(x_buf[0][:, :], p_l1[:, :], x_buf[0][:, :],
                                  ALU.add).then_inc(x1_added, 1)

            def add_acc(s, c, l2_tiles):
                dve.wait_ge(x1_added, c + 1)
                if not (isinstance(c, int) and c == 0):
                    dve.wait_ge(acc_stored, 16 * c)
                if s == 0:
                    dve.tensor_copy(acc_buf[:, :], x_buf[0][:, :]).then_inc(acc_added, 1)
                else:
                    dve.wait_ge(q_used, l2_tiles)
                    dve.tensor_tensor(acc_buf[:, :], p_l2[0][:, :], x_buf[0][:, :],
                                      ALU.add).then_inc(acc_added, 1)

            for i in range(NC):
                premask(0, 0, i)
                centre(i, i % 2, i % 3, i % 4)
                if i >= 2:
                    square(i - 2, (i - 2) % S_RING)
                    norm_relu(i - 2, i % 2, (i - 2) % 3, True)
                if i >= 4:
                    keep_h1(i - 4)
            for n in (NC - 2, NC - 1):
                norm_relu(n, n % 2, n % 3, True)
                keep_h1(n - 2)
            keep_h1(NC - 2)
            keep_h1(NC - 1)

            def chunk(s, c):
                before = (c - 1) // GROUP if isinstance(c, int) else s
                for i in range(NC):
                    premask(s, c, i)
                    if i == 3:
                        add_x1(c - 1)
                    square(c * NC + i - 2, (i - 2) % S_RING)
                    if i == 4:
                        add_acc(before, c - 1, l2_before(s, c, 0))
                    if i == 5:
                        centre(c + NC - 1, 0, 0, 0)
                    if i == 9:
                        norm_relu(c + NC - 1, 0, 0, False)
                    if i == 11:
                        keep_h2(c - 1)

            phase1_chunks(dve, chunk)
            square(PH1 - 2, (NC - 2) % S_RING)
            square(PH1 - 1, (NC - 1) % S_RING)
            add_x1(NC - 1)
            add_acc(NG - 1, NC - 1, L2_BASE[NG])
            centre(2 * NC - 1, 0, 0, 0)
            norm_relu(2 * NC - 1, 0, 0, False)
            keep_h2(NC - 1)

            def finish(s, c, c0, par):
                dve.wait_ge(s_used, PH1 + ph2_before(s, c, PH2_N[s]))
                dve.wait_ge(acc_loaded[par], 8 * c0 + 16)
                if not (isinstance(c0, int) and c0 == 0):
                    dve.wait_ge(out_stored[par], 8 * c0)
                dve.tensor_tensor(out_buf[par][:, :], p_l2[1 - par][:, :], acc_in[par][:, :],
                                  ALU.add).then_inc(final_done, 1)

            def pair(s, c0):
                for par in range(2):
                    finish(s, c0 + par, c0, par)

            phase2_pairs(dve, pair)

        @block.scalar
        def _(act):
            act.preload_act_table_set("natural_log_exp_and_others")
            act.wait_ge(param_step, 3)

            def log(c, i):
                act.wait_ge(premasked, c * NC + i + 1)
                v = s_tile(i % S_RING)
                act.activation(v, v, ACT.Ln, bias=tiny_c).then_inc(ln_done, 1)

            def reciprocal(t, slot):
                act.wait_ge(ln_done, t + 1)
                v = s_tile(slot)
                act.activation(v, v, ACT.Exp, scale=-1.0).then_inc(recip_done, 1)

            def sensitivity(t, slot):
                act.wait_ge(squared, t + 1)
                v = s_tile(slot)
                act.activation(v, v, ACT.Exp, bias=exp_bias, scale=neg_k).then_inc(sens_done, 1)

            def rstd(n, b, stat, apart):
                act.wait_ge(var_done, n + 1)
                if not (isinstance(n, int) and n < 2):
                    act.wait_ge(normed, n - 1 if apart else n)
                act.activation(rstd_buf[b][:, :], p_stat[stat][:, :], ACT.Ln,
                               bias=eps_c).then_inc(log_var_done, 1)
                act.wait_ge(log_var_done, n + 1)
                act.activation(rstd_buf[b][:, :], rstd_buf[b][:, :], ACT.Exp,
                               scale=-0.5).then_inc(rstd_done, 1)

            for i in range(NC):
                log(0, i)
                if i >= 1:
                    reciprocal(i - 1, (i - 1) % S_RING)
                    rstd(i - 1, (i - 1) % 2, (i - 1) % 4, True)
                if i == 2:
                    act.wait_ge(param_step, 11)
                if i >= 2:
                    sensitivity(i - 2, (i - 2) % S_RING)
            rstd(NC - 1, 1, 3, True)

            def chunk(s, c):
                for i in range(NC):
                    log(c, i)
                    reciprocal(c * NC + i - 1, (i - 1) % S_RING)
                    sensitivity(c * NC + i - 2, (i - 2) % S_RING)
                    if i == 8:
                        rstd(c + NC - 1, 0, 0, False)

            phase1_chunks(act, chunk)
            reciprocal(PH1 - 1, (NC - 1) % S_RING)
            sensitivity(PH1 - 2, (NC - 2) % S_RING)
            sensitivity(PH1 - 1, (NC - 1) % S_RING)

            def pair(s, c0):
                for par in range(2):
                    c = c0 + par
                    for k in range(PH2_N[s]):
                        n = ph2_before(s, c, k)
                        slot = (par * PH2_N[s] + k) % S_RING
                        act.wait_ge(a_loaded[k % A_RING],
                                    16 * (PH1 // A_RING + 1 + k // A_RING)
                                    + (16 // A_RING) * (PH2_BASE[s] + (c - GROUP * s) * PH2_N[s]))
                        act.wait_ge(s_used, PH1 + n - S_RING + 1)
                        act.activation(s_tile(slot), a_tile(k % A_RING),
                                       ACT.Square).then_inc(sq2_ready, 1)
                        if isinstance(c, int) and c == 0 and k == 7:
                            rstd(2 * NC - 1, 0, 0, False)

            phase2_pairs(act, pair)

        @block.gpsimd
        def _(pool):
            pool.wait_ge(strip_zeroed, 1)
            eye = eye_strip[:, (GROUP - 1) * P:GROUP * P]
            pool.affine_select(out=eye, in_=eye, compare_op=ALU.not_equal, fill=1.0, base=0,
                               pattern=[[-1, P]], channel_multiplier=1).then_inc(strip_ready, 1)

            def square_deviation(n, b, cb, apart):
                pool.wait_ge(centred, n + 1)
                if not (isinstance(n, int) and n < 2):
                    pool.wait_ge(var_done, n - 1 if apart else n)
                pool.tensor_tensor(square_buf[b][:, :], centred_buf[cb][:, :], centred_buf[cb][:, :],
                                   ALU.mult).then_inc(dev_squared, 1)

            for n in range(NC):
                square_deviation(n, n % 2, n % 3, True)

            def square_adj(s, c, i):
                n, r = l2_before(s, c, i), L2_RANK[s][i]
                pool.wait_ge(a_loaded[i % A_RING], 16 * (c * (NC // A_RING) + i // A_RING + 1))
                if not (isinstance(n, int) and n < Q_RING):
                    pool.wait_ge(q_used, n - Q_RING + 1)
                a = a_tile(i % A_RING)
                pool.tensor_tensor(q_tile(r % Q_RING), a, a, ALU.mult).then_inc(q_ready, 1)

            def chunk(s, c):
                for i in range(NC):
                    if i == 6:
                        square_deviation(c + NC - 1, 0, 0, False)
                    if ORDER[s][i] < GROUP * s:
                        square_adj(s, c, i)

            phase1_chunks(pool, chunk)

            def load_acc(c, par, finished):
                pool.wait_ge(acc_stored, 16 * (c + 1))
                if finished is not None:
                    pool.wait_ge(final_done, finished)
                pool.dma_start(acc_in[par][:, :], columns(acc_dram, c)).then_inc(acc_loaded[par], 16)

            def store_out(c, par):
                pool.wait_ge(final_done, c + 1)
                pool.dma_start(columns(outT, c), out_buf[par][:, :]).then_inc(out_stored[par], 16)

            def add_eye(s, c, par):
                for k in range(GROUP):
                    if isinstance(c, int) and c == 0 and k == 2:
                        square_deviation(2 * NC - 1, 0, 0, False)
                    pool.wait_ge(sq2_ready, ph2_before(s, c, k) + 1)
                    d = diagonal(s_ring, (par * PH2_N[s] + k) % S_RING)
                    pool.tensor_tensor(d, d, eye_if_diagonal(GROUP * s + k, c, s),
                                       ALU.add).then_inc(eye_added, 1)

            def pair(s, c0):
                for par in range(2):
                    c = c0 + par
                    add_eye(s, c, par)
                    if isinstance(c, int) and c == 0:
                        pool.wait_ge(normed, 2 * NC)
                        load_acc(0, 0, None)
                        load_acc(1, 1, None)
                        continue
                    store_out(c - 1, 1 - par)
                    if not (isinstance(c, int) and c == NC - 1):
                        load_acc(c + 1, 1 - par, c)

            phase2_pairs(pool, pair, last_apart=True)
            store_out(NC - 1, 1)
            for par in range(2):
                pool.wait_ge(out_stored[par], 16 * (NC // 2))


def kernel(x, adj, L0_gnn_W, L0_gnn_B, L0_gnn_mu, L0_gnn_sigma, L1_gnn_W):
    import numpy as np
    import concourse.bacc as bacc
    from concourse.bass_utils import run_bass_kernel_spmd

    tiles = np.asarray(adj).reshape(NC, CHUNK, NC, G, P).transpose(0, 2, 4, 3, 1)
    arrays = {
        "xT": np.ascontiguousarray(np.asarray(x).T),
        "adjT": np.ascontiguousarray(tiles).reshape(NC * NC, P, TILE),
        "W0": np.ascontiguousarray(L0_gnn_W),
        "B0": np.ascontiguousarray(L0_gnn_B),
        "mu": np.ascontiguousarray(L0_gnn_mu),
        "sigma": np.ascontiguousarray(L0_gnn_sigma),
        "W1T": np.ascontiguousarray(np.asarray(L1_gnn_W).T),
    }
    nc = bacc.Bacc("TRN2", target_bir_lowering=False, num_devices=1)
    args = [nc.dram_tensor(name, a.shape, mybir.dt.from_np(a.dtype), kind="ExternalInput").ap()
            for name, a in arrays.items()]
    outT = nc.dram_tensor("outT", (D, N), F32, kind="ExternalOutput").ap()
    gnn_program(nc, *args, outT)
    r = run_bass_kernel_spmd(nc, [arrays], core_ids=[0])
    return np.ascontiguousarray(r.results[0]["outT"].T)
```

```python
from contextlib import ExitStack

import concourse.bass as bass
from concourse import mybir

ALU = mybir.AluOpType
ACT = mybir.ActivationFunctionType
F32 = mybir.dt.float32
F32R = mybir.dt.float32r

P = 128
D = 128
N = 8192
CHUNK = 512
NC = N // CHUNK
G = CHUNK // P
TILE = G * CHUNK
GROUP = 4
NG = NC // GROUP
A_RING = 4
S_RING = 8
Q_RING = 2
R_RING = 4
DIAG = CHUNK + P
LN_EPS = 1e-5
CUTOFF = 0.5
TINY = 2.0 ** -60


def order_of(s):
    with_l2, without = iter(range(GROUP * s)), iter(range(GROUP * s, NC))
    n = GROUP * s
    return [next(with_l2) if (i + 1) * n // NC > i * n // NC else next(without) for i in range(NC)]


ORDER = [order_of(s) for s in range(NG)]
L2_BASE = [sum(GROUP * GROUP * r for r in range(s)) for s in range(NG + 1)]
L2_RANK = [[sum(J < GROUP * s for J in ORDER[s][:i]) for i in range(NC + 1)] for s in range(NG)]
PH1 = NC * NC
PH2_N = [NC - GROUP * s for s in range(NG)]
PH2_BASE = [GROUP * sum(PH2_N[:s]) for s in range(NG)]


def l2_before(s, c, i):
    return L2_BASE[s] + (c - GROUP * s) * (GROUP * s) + L2_RANK[s][i]


def l2_before_back(s, c, i, back):
    if i >= back:
        return l2_before(s, c, i - back)
    if isinstance(c, int):
        return l2_before((c - 1) // GROUP, c - 1, i - back + NC) if c else 0
    return l2_before(s, c - 1, i - back + NC)


def ph2_before(s, c, k):
    return PH2_BASE[s] + (c - GROUP * s) * PH2_N[s] + k


def ph2_half(s, c, k):
    return PH2_BASE[s] // 2 + (c - GROUP * s) * (PH2_N[s] // 2) + k // 2


def phase1_chunks(eng, body):
    for s in range(NG):
        first = max(1, GROUP * s)
        body(s, first)
        with eng.Fori(first + 1, GROUP * (s + 1)) as c:
            body(s, c)


def phase2_pairs(eng, body, first_apart=False, last_apart=False):
    for s in range(NG):
        lo, hi = GROUP * s, GROUP * (s + 1)
        if s == 0 or first_apart or (s == NG - 1 and last_apart):
            for c in range(lo, hi, 2):
                body(s, c)
        else:
            with eng.Fori(lo // 2, hi // 2) as half:
                body(s, half * 2)


def gnn_program(nc, xT, adjT, W0, B0, mu, sigma, W1T, outT):
    with ExitStack() as ctx:
        def sb(name, shape):
            return ctx.enter_context(nc.sbuf_tensor(name, shape, F32))

        def bank(name):
            return ctx.enter_context(nc.psum_tensor(name, [P, CHUNK], F32))

        def sem(name):
            return ctx.enter_context(nc.semaphore(name))

        acc_dram = nc.dram_tensor("acc_dram", [D, N], F32).ap()

        h_size, s_size, q_size = NC * G * D, S_RING * TILE, Q_RING * TILE
        arena_size = 4 * (2 * h_size + s_size + q_size)
        ctx.enter_context(nc.sbuf_tensor("arena", [P, arena_size // 4], F32))
        arena = nc.sbuf_base - arena_size

        def at(name, shape, words, dtype=F32):
            return nc.alloc_sbuf_tensor_at(name, shape, dtype, offset=arena + 4 * words)

        h1 = at("h1", [P, NC * G, D], 0)
        h2 = at("h2", [P, NC * G, D], h_size)
        s_ring = at("s_ring", [P, s_size], 2 * h_size)
        q_ring = at("q_ring", [P, q_size], 2 * h_size + s_size)
        h2_high = at("h2_high", [P, NC * G, D], 0, F32R)
        h2_low = at("h2_low", [P, NC * G, D], h_size, F32R)
        high_ring = at("high_ring", [P, R_RING * TILE], 2 * h_size, F32R)
        low_ring = at("low_ring", [P, R_RING * TILE], 2 * h_size + R_RING * TILE, F32R)
        square_ring = at("square_ring", [P, R_RING * TILE], 2 * h_size + R_RING * TILE)

        a_ring = sb("a_ring", [P, A_RING * TILE + CHUNK])
        x_buf = [sb(f"x_buf{n}", [D, CHUNK]) for n in range(2)]
        centred_buf = [sb(f"centred_buf{n}", [D, CHUNK]) for n in range(3)]
        square_buf = [sb(f"square_buf{n}", [D, CHUNK]) for n in range(2)]
        rstd_buf = [sb(f"rstd_buf{n}", [D, CHUNK]) for n in range(2)]
        normed_buf = [sb(f"normed_buf{n}", [D, CHUNK]) for n in range(2)]
        acc_buf = square_buf[1]
        acc_in = rstd_buf
        out_buf = normed_buf
        bias_rows = sb("bias_rows", [P, D])
        w0 = sb("w0", [D, D])
        w1 = sb("w1", [D, D])
        mean_of = sb("mean_of", [D, D])
        eye_strip = sb("eye_strip", [P, (2 * GROUP - 1) * P])
        small = sb("small", [P, 16])
        mu_c, sigma_c, inv_mu, neg_2c, var2, inv_var2, neg_k, c_sq, exp_bias, tiny_c, eps_c = (
            small[:, n:n + 1] for n in range(11))

        p_l1 = bank("p_l1")
        p_l2 = [bank("p_l2a"), bank("p_l2b")]
        p_stat = [bank("p_stat0"), bank("p_stat1"), bank("p_stat2"), p_l2[1]]
        p_proj = [bank("p_proj0"), bank("p_proj1")]

        a_loaded = [sem(f"a_loaded{n}") for n in range(A_RING)]
        x_loaded = [sem("x_loaded0"), sem("x_loaded1")]
        weights_loaded = sem("weights_loaded")
        params_loaded = sem("params_loaded")
        param_step = sem("param_step")
        strip_zeroed = sem("strip_zeroed")
        strip_ready = sem("strip_ready")
        diag_marked = sem("diag_marked")
        premasked = sem("premasked")
        ln_done = sem("ln_done")
        recip_done = sem("recip_done")
        squared = sem("squared")
        sens_done = sem("sens_done")
        s_used = sem("s_used")
        q_ready = sem("q_ready")
        q_used = sem("q_used")
        x1_added = sem("x1_added")
        acc_added = sem("acc_added")
        acc_complete = sem("acc_complete")
        acc_stored = sem("acc_stored")
        mean_done = sem("mean_done")
        centred = sem("centred")
        dev_squared = sem("dev_squared")
        var_done = sem("var_done")
        log_var_done = sem("log_var_done")
        rstd_done = sem("rstd_done")
        normed = sem("normed")
        projected = sem("projected")
        h_ready = sem("h_ready")
        h_split = sem("h_split")
        h_high_done = sem("h_high_done")
        high_ready = sem("high_ready")
        pool_square = sem("pool_square")
        act_square = sem("act_square")
        low_ready = sem("low_ready")
        final_done = sem("final_done")
        acc_loaded = [sem("acc_loaded0"), sem("acc_loaded1")]
        out_stored = [sem("out_stored0"), sem("out_stored1")]

        def tile(ring, slot):
            return ring[:, slot * TILE:(slot + 1) * TILE]

        def a_tile(slot):
            return tile(a_ring, slot)

        def s_tile(slot):
            return tile(s_ring, slot)

        def diagonal(ring, slot):
            v = ring[:, slot * TILE:slot * TILE + G * DIAG]
            return v.rearrange("p (g n) -> p g n", g=G)[:, :, 0:P]

        def eye_if_diagonal(J, c, s):
            first = c * P + (GROUP - 1 - J) * P
            return eye_strip[:, bass.ds(first, P)].unsqueeze(1).to_broadcast([P, G, P])

        def adj_tile(c, J):
            return adjT[bass.ds(c * NC + J, 1), :, :].rearrange("t p n -> p (t n)")

        def columns(dram, c):
            return dram[:, bass.ds(c * CHUNK, CHUNK)]

        block = ctx.enter_context(nc.Block())

        @block.sync
        def _(sp):
            def load_tile(s, c, i):
                J, t = ORDER[s][i], c * NC + i
                if not (isinstance(c, int) and t < A_RING):
                    n = l2_before_back(s, c, i, A_RING - 1)
                    if not isinstance(n, int):
                        sp.compute_val(n)
                    sp.wait_ge(premasked, t - A_RING + 1)
                    if not (isinstance(n, int) and n == 0):
                        sp.wait_ge(q_ready, n)
                sp.dma_start(a_tile(i % A_RING), adj_tile(c, J)).then_inc(a_loaded[i % A_RING], 16)

            def load_x(n):
                if n >= 2:
                    sp.wait_ge(centred, n - 1)
                sp.dma_start(x_buf[n % 2][:, :], columns(xT, n)).then_inc(x_loaded[n % 2], 16)

            load_x(0)
            sp.dma_start(mu_c, mu.partition_broadcast(P)).then_inc(params_loaded, 16)
            sp.dma_start(sigma_c, sigma.partition_broadcast(P)).then_inc(params_loaded, 16)
            load_tile(0, 0, 0)
            sp.dma_start(w0[:, :], W0).then_inc(weights_loaded, 16)
            sp.dma_start(w1[:, :], W1T).then_inc(weights_loaded, 16)
            sp.dma_start(bias_rows[:, :], B0.partition_broadcast(P)).then_inc(weights_loaded, 16)
            load_x(1)
            for i in range(1, NC):
                load_tile(0, 0, i)
                if 2 <= i:
                    load_x(i)

            def store_acc(c):
                sp.wait_ge(acc_complete, c + 1)
                sp.dma_start(columns(acc_dram, c), acc_buf[:, :]).then_inc(acc_stored, 16)

            def chunk(s, c):
                for i in range(NC):
                    load_tile(s, c, i)
                    if i == 3:
                        sp.wait_ge(centred, c + NC - 1)
                        sp.dma_start(x_buf[0][:, :], columns(xT, c - 1)).then_inc(x_loaded[0], 16)
                    if i == 1 and not (isinstance(c, int) and c == 1):
                        store_acc(c - 2)

            phase1_chunks(sp, chunk)
            sp.wait_ge(centred, 2 * NC - 1)
            sp.dma_start(x_buf[0][:, :], columns(xT, NC - 1)).then_inc(x_loaded[0], 16)
            store_acc(NC - 2)

            def load_tile2(s, c, k):
                n = ph2_before(s, c, k)
                if isinstance(n, int) and n < A_RING:
                    sp.wait_ge(premasked, PH1 + n - A_RING + 1)
                    sp.wait_ge(q_ready, l2_before(NG - 1, NC - 1, NC + n - A_RING + 1))
                else:
                    if k % 2 == 0:
                        pool_squares = ph2_half(s, c, k) - A_RING // 2 + 1
                        if not isinstance(n, int):
                            sp.compute_val(pool_squares)
                    sp.wait_ge(high_ready, n - A_RING + 1)
                    if k % 2 == 0:
                        sp.wait_ge(pool_square, pool_squares)
                sp.dma_start(a_tile(k % A_RING), adj_tile(c, GROUP * s + k)).then_inc(
                    a_loaded[k % A_RING], 16)

            def pair(s, c0):
                for c in (c0, c0 + 1):
                    for k in range(PH2_N[s]):
                        load_tile2(s, c, k)
                        if isinstance(c, int) and c == 1 and k == 0:
                            store_acc(NC - 1)

            phase2_pairs(sp, pair)

        @block.tensor
        def _(pe):
            def l1(s, c, i):
                J, t = ORDER[s][i], c * NC + i
                if isinstance(c, int) and c == 0:
                    pe.wait_ge(h_ready, J + 1)
                elif i == 0:
                    pe.wait_ge(x1_added, c)
                pe.wait_ge(sens_done, t + 1)
                for g in range(G):
                    last = pe.matmul(p_l1[:, :], h1[:, J * G + g, :],
                                     s_tile(i % S_RING)[:, g * CHUNK:(g + 1) * CHUNK],
                                     start=(i == 0 and g == 0), stop=(i == NC - 1 and g == G - 1))
                last.then_inc(s_used, 1)

            def l2(s, c, i):
                J, r = ORDER[s][i], L2_RANK[s][i]
                if r == 0:
                    pe.wait_ge(acc_added, c)
                pe.wait_ge(h_ready, NC + J + 1)
                pe.wait_ge(q_ready, l2_before(s, c, i) + 1)
                for g in range(G):
                    last = pe.matmul(p_l2[0][:, :], h2[:, J * G + g, :],
                                     tile(q_ring, r % Q_RING)[:, g * CHUNK:(g + 1) * CHUNK],
                                     start=(r == 0 and g == 0),
                                     stop=(r == GROUP * s - 1 and g == G - 1))
                last.then_inc(q_used, 1)

            def mean(n, b):
                if b is None:
                    pe.wait_ge(rstd_done, n)
                elif n >= 4:
                    pe.wait_ge(rstd_done, n - 3)
                if b is not None:
                    pe.wait_ge(x_loaded[b], 16 * (n // 2 + 1))
                sb_ = 0 if b is None else n % 4
                b = b or 0
                pe.matmul(p_stat[sb_][:, :], mean_of[:, :], x_buf[b][:, :], start=True,
                          stop=True).then_inc(mean_done, 1)

            def variance(n, b, stat):
                pe.wait_ge(dev_squared, n + 1)
                pe.matmul(p_stat[stat][:, :], mean_of[:, :], square_buf[b][:, :], start=True,
                          stop=True).then_inc(var_done, 1)

            def project(n, b, w, apart):
                pe.wait_ge(normed, n + 1)
                if not apart:
                    if not (isinstance(n, int) and n == NC):
                        pe.wait_ge(acc_complete, n - NC)
                    pe.matmul(p_proj[1][:, :], w[:, :], normed_buf[b][:, :], start=True, stop=True)
                if not (isinstance(n, int) and n < 2):
                    pe.wait_ge(h_ready, n - 1 if apart else n)
                for g in range(G):
                    last = pe.matmul(p_proj[b][:, g * P:(g + 1) * P],
                                     normed_buf[b][:, g * P:(g + 1) * P], w[:, :],
                                     start=True, stop=True)
                last.then_inc(projected, 1)

            pe.wait_ge(param_step, 2)
            mean(0, 0)
            for m in range(NC + 3):
                if m + 1 < NC:
                    mean(m + 1, (m + 1) % 2)
                if m >= 5:
                    l1(0, 0, m - 5)
                if m < NC:
                    variance(m, m % 2, m % 4)
                if m == 3:
                    pe.wait_ge(weights_loaded, 48)
                if m >= 3:
                    project(m - 3, (m - 3) % 2, w0, True)
            for i in (NC - 2, NC - 1):
                l1(0, 0, i)

            def chunk(s, c):
                for i in range(NC):
                    l1(s, c, i)
                    if i == 0:
                        mean(c + NC - 1, None)
                    if ORDER[s][i] < GROUP * s:
                        l2(s, c, i)
                    if i == 3:
                        variance(c + NC - 1, 0, 0)
                    if i == 6:
                        project(c + NC - 1, 0, w1, False)

            phase1_chunks(pe, chunk)

            def l2_rest(s, c, par, k):
                J, n = GROUP * s + k, ph2_before(s, c, k)
                if isinstance(c, int) and c == 0:
                    pe.wait_ge(h_split, J + 1)
                pe.wait_ge(low_ready, n + 1)
                for g in range(G):
                    columns_of_g = slice(k % R_RING * TILE + g * CHUNK,
                                         k % R_RING * TILE + (g + 1) * CHUNK)
                    high, low = high_ring[:, columns_of_g], low_ring[:, columns_of_g]
                    parts = ((h2_high, high), (h2_high, low), (h2_low, high))
                    for m, (h, q) in enumerate(parts):
                        last = pe.matmul(p_l2[1 - par][:, :], h[:, J * G + g, :], q,
                                         start=(k == 0 and g == 0 and m == 0),
                                         stop=(k == PH2_N[s] - 1 and g == G - 1
                                               and m == len(parts) - 1))
                last.then_inc(s_used, 1)

            def pair(s, c0):
                for par in range(2):
                    c = c0 + par
                    if isinstance(c, int) and c == 1:
                        pe.wait_ge(acc_added, NC)
                    if not (isinstance(c, int) and c < 2):
                        pe.wait_ge(final_done, c - 1)
                    for k in range(PH2_N[s]):
                        if isinstance(c, int) and c == 0 and k == 0:
                            pe.wait_ge(x1_added, NC)
                            mean(2 * NC - 1, None)
                        l2_rest(s, c, par, k)
                        if isinstance(c, int) and c == 0:
                            if k == 1:
                                variance(2 * NC - 1, 0, 0)
                            if k == 8:
                                project(2 * NC - 1, 0, w1, False)

            phase2_pairs(pe, pair)

        @block.vector
        def _(dve):
            steps = [0]

            def small_step(instruction):
                steps[0] += 1
                instruction.then_inc(param_step, 1)
                dve.wait_ge(param_step, steps[0])

            dve.memset(eye_strip[:, :], 0.0).then_inc(strip_zeroed, 1)
            small_step(dve.memset(tiny_c, TINY))
            small_step(dve.memset(mean_of[:, :], 1.0 / D))
            small_step(dve.memset(eps_c, LN_EPS))
            dve.wait_ge(params_loaded, 32)
            small_step(dve.reciprocal(inv_mu, mu_c))
            small_step(dve.tensor_scalar(neg_2c, inv_mu, -2.0, None, ALU.mult))
            small_step(dve.tensor_tensor(var2, sigma_c, sigma_c, ALU.mult))
            small_step(dve.tensor_scalar(var2, var2, 2.0, None, ALU.mult))
            small_step(dve.reciprocal(inv_var2, var2))
            small_step(dve.tensor_scalar(neg_k, inv_var2, -1.0, None, ALU.mult))
            small_step(dve.tensor_tensor(c_sq, inv_mu, inv_mu, ALU.mult))
            small_step(dve.tensor_tensor(exp_bias, c_sq, neg_k, ALU.mult))
            dve.wait_ge(strip_ready, 1)

            def premask(s, c, i):
                J, t = ORDER[s][i], c * NC + i
                dve.wait_ge(a_loaded[i % A_RING], 16 * (c * (NC // A_RING) + i // A_RING + 1))
                if GROUP * s <= J < GROUP * (s + 1):
                    d = diagonal(a_ring, i % A_RING)
                    dve.tensor_tensor(d, d, eye_if_diagonal(J, c, s), ALU.add).then_inc(diag_marked, 1)
                    dve.wait_ge(diag_marked, c * GROUP + J - GROUP * s + 1)
                if not (isinstance(c, int) and t < S_RING):
                    dve.wait_ge(s_used, t - S_RING + 1)
                dve.scalar_tensor_tensor(out=s_tile(i % S_RING), in0=a_tile(i % A_RING), scalar=CUTOFF,
                                         in1=a_tile(i % A_RING), op0=ALU.is_lt,
                                         op1=ALU.mult).then_inc(premasked, 1)

            def square(t, slot):
                dve.wait_ge(recip_done, t + 1)
                v = s_tile(slot)
                dve.scalar_tensor_tensor(out=v, in0=v, scalar=neg_2c, in1=v, op0=ALU.add,
                                         op1=ALU.mult).then_inc(squared, 1)

            def centre(n, b, cb, stat):
                if isinstance(n, int) and 3 <= n < NC:
                    dve.wait_ge(normed, n - 2)
                dve.wait_ge(mean_done, n + 1)
                dve.tensor_tensor(centred_buf[cb][:, :], x_buf[b][:, :], p_stat[stat][:, :],
                                  ALU.subtract).then_inc(centred, 1)

            def norm_relu(n, b, cb, apart):
                dve.wait_ge(rstd_done, n + 1)
                if not (isinstance(n, int) and n < 2):
                    dve.wait_ge(projected, n - 1 if apart else n)
                dve.scalar_tensor_tensor(out=normed_buf[b][:, :], in0=centred_buf[cb][:, :], scalar=0.0,
                                         in1=rstd_buf[b][:, :], op0=ALU.max,
                                         op1=ALU.mult).then_inc(normed, 1)

            def keep_h1(n):
                dve.wait_ge(projected, n + 1)
                if n == 0:
                    dve.wait_ge(weights_loaded, 48)
                dve.tensor_tensor(h1[:, n * G:(n + 1) * G, :],
                                  p_proj[n % 2][:, :].rearrange("p (g n) -> p g n", g=G),
                                  bias_rows[:, :].unsqueeze(1).to_broadcast([P, G, D]),
                                  ALU.add).then_inc(h_ready, 1)

            def complete_acc(c):
                dve.wait_ge(projected, c + NC + 1)
                dve.wait_ge(acc_added, c + 1)
                dve.tensor_tensor(acc_buf[:, :], p_proj[1][:, :], acc_buf[:, :],
                                  ALU.add).then_inc(acc_complete, 1)

            def keep_h2(c):
                dve.wait_ge(projected, c + NC + 1)
                dve.tensor_copy(h2[:, bass.ds(c * G, G), :],
                                p_proj[0][:, :].rearrange("p (g n) -> p g n", g=G)).then_inc(h_ready, 1)

            def add_x1(c):
                dve.wait_ge(s_used, (c + 1) * NC)
                dve.wait_ge(x_loaded[0], 16 * (c + NC // 2 + 1))
                dve.tensor_tensor(x_buf[0][:, :], p_l1[:, :], x_buf[0][:, :],
                                  ALU.add).then_inc(x1_added, 1)

            def add_acc(s, c, l2_tiles):
                dve.wait_ge(x1_added, c + 1)
                if not (isinstance(c, int) and c == 0):
                    dve.wait_ge(acc_stored, 16 * c)
                if s == 0:
                    dve.tensor_copy(acc_buf[:, :], x_buf[0][:, :]).then_inc(acc_added, 1)
                else:
                    dve.wait_ge(q_used, l2_tiles)
                    dve.tensor_tensor(acc_buf[:, :], p_l2[0][:, :], x_buf[0][:, :],
                                      ALU.add).then_inc(acc_added, 1)

            for i in range(NC):
                premask(0, 0, i)
                centre(i, i % 2, i % 3, i % 4)
                if i >= 2:
                    square(i - 2, (i - 2) % S_RING)
                    norm_relu(i - 2, i % 2, (i - 2) % 3, True)
                if i >= 4:
                    keep_h1(i - 4)
            for n in (NC - 2, NC - 1):
                norm_relu(n, n % 2, n % 3, True)
                keep_h1(n - 2)
            keep_h1(NC - 2)
            keep_h1(NC - 1)

            def chunk(s, c):
                before = (c - 1) // GROUP if isinstance(c, int) else s
                for i in range(NC):
                    premask(s, c, i)
                    if i == 3:
                        add_x1(c - 1)
                    square(c * NC + i - 2, (i - 2) % S_RING)
                    if i == 4:
                        add_acc(before, c - 1, l2_before(s, c, 0))
                    if i == 5:
                        centre(c + NC - 1, 0, 0, 0)
                    if i == 9:
                        norm_relu(c + NC - 1, 0, 0, False)
                    if i == 11:
                        keep_h2(c - 1)
                    if i == 12:
                        complete_acc(c - 1)

            phase1_chunks(dve, chunk)
            square(PH1 - 2, (NC - 2) % S_RING)
            square(PH1 - 1, (NC - 1) % S_RING)

            def split_h2(J):
                at_step = ORDER[NG - 1].index(J)
                dve.wait_ge(s_used, PH1 - NC + at_step + 1)
                if J < GROUP * (NG - 1):
                    dve.wait_ge(q_used, l2_before(NG - 1, NC - 1, at_step) + 1)
                if J == NC - 1:
                    dve.wait_ge(h_ready, 2 * NC)
                rows = slice(J * G, (J + 1) * G)
                dve.tensor_copy(h2_high[:, rows, :], h2[:, rows, :]).then_inc(h_high_done, 1)
                dve.wait_ge(h_high_done, J + 1)
                dve.tensor_tensor(h2_low[:, rows, :], h2[:, rows, :],
                                  h2_high[:, rows, :].bitcast(F32), ALU.subtract).then_inc(h_split, 1)

            def low(s, c, k):
                dve.wait_ge(high_ready, ph2_before(s, c, k) + 1)
                if k % 2 == 0:
                    dve.wait_ge(pool_square, ph2_half(s, c, k) + 1)
                slot = k % R_RING
                dve.tensor_tensor(tile(low_ring, slot), tile(square_ring, slot),
                                  tile(high_ring, slot).bitcast(F32), ALU.subtract).then_inc(low_ready, 1)

            def finish(s, c, par, stored):
                dve.wait_ge(s_used, PH1 + ph2_before(s, c, PH2_N[s]))
                dve.wait_ge(acc_loaded[par], stored + 16)
                if not (isinstance(stored, int) and stored == 0):
                    dve.wait_ge(out_stored[par], stored)
                dve.tensor_tensor(out_buf[par][:, :], p_l2[1 - par][:, :], acc_in[par][:, :],
                                  ALU.add).then_inc(final_done, 1)

            def pair(s, c0):
                for par in range(2):
                    c = c0 + par
                    for k in range(PH2_N[s]):
                        low(s, c, k)
                        if k == 2 and not (isinstance(c, int) and c == 0):
                            before = (c - 1) // GROUP if isinstance(c, int) else s
                            finish(before, c - 1, 1 - par, 8 * (c0 - 2) + 16 * par)
                        if isinstance(c, int) and c == 0:
                            last_job(k)

            def last_job(k):
                if k == 0:
                    centre(2 * NC - 1, 0, 0, 0)
                    split_h2(4)
                    split_h2(5)
                if k == 1:
                    add_acc(NG - 1, NC - 1, L2_BASE[NG])
                    split_h2(6)
                    split_h2(7)
                if 2 <= k <= 5:
                    split_h2(2 * k + 4)
                    if k < 5:
                        split_h2(2 * k + 5)
                if k == 7:
                    norm_relu(2 * NC - 1, 0, 0, False)
                if k == 9:
                    keep_h2(NC - 1)
                    split_h2(NC - 1)
                    complete_acc(NC - 1)

            for J in range(4):
                split_h2(J)
            add_x1(NC - 1)
            phase2_pairs(dve, pair, first_apart=True)
            finish(NG - 1, NC - 1, 1, 16 * (NC // 2 - 1))

        @block.scalar
        def _(act):
            act.preload_act_table_set("natural_log_exp_and_others")
            act.wait_ge(param_step, 3)

            def log(c, i):
                act.wait_ge(premasked, c * NC + i + 1)
                v = s_tile(i % S_RING)
                act.activation(v, v, ACT.Ln, bias=tiny_c).then_inc(ln_done, 1)

            def reciprocal(t, slot):
                act.wait_ge(ln_done, t + 1)
                v = s_tile(slot)
                act.activation(v, v, ACT.Exp, scale=-1.0).then_inc(recip_done, 1)

            def sensitivity(t, slot):
                act.wait_ge(squared, t + 1)
                v = s_tile(slot)
                act.activation(v, v, ACT.Exp, bias=exp_bias, scale=neg_k).then_inc(sens_done, 1)

            def rstd(n, b, stat, apart):
                act.wait_ge(var_done, n + 1)
                if not (isinstance(n, int) and n < 2):
                    act.wait_ge(normed, n - 1 if apart else n)
                act.activation(rstd_buf[b][:, :], p_stat[stat][:, :], ACT.Ln,
                               bias=eps_c).then_inc(log_var_done, 1)
                act.wait_ge(log_var_done, n + 1)
                act.activation(rstd_buf[b][:, :], rstd_buf[b][:, :], ACT.Exp,
                               scale=-0.5).then_inc(rstd_done, 1)

            for i in range(NC):
                log(0, i)
                if i >= 1:
                    reciprocal(i - 1, (i - 1) % S_RING)
                    rstd(i - 1, (i - 1) % 2, (i - 1) % 4, True)
                if i == 2:
                    act.wait_ge(param_step, 11)
                if i >= 2:
                    sensitivity(i - 2, (i - 2) % S_RING)
            rstd(NC - 1, 1, 3, True)

            def chunk(s, c):
                for i in range(NC):
                    log(c, i)
                    reciprocal(c * NC + i - 1, (i - 1) % S_RING)
                    sensitivity(c * NC + i - 2, (i - 2) % S_RING)
                    if i == 8:
                        rstd(c + NC - 1, 0, 0, False)

            phase1_chunks(act, chunk)
            reciprocal(PH1 - 1, (NC - 1) % S_RING)
            sensitivity(PH1 - 2, (NC - 2) % S_RING)
            sensitivity(PH1 - 1, (NC - 1) % S_RING)

            def load_acc(c, par, finished):
                act.wait_ge(acc_stored, 16 * (c + 1))
                if finished is not None:
                    act.wait_ge(final_done, finished)
                act.dma_start(acc_in[par][:, :], columns(acc_dram, c)).then_inc(acc_loaded[par], 16)

            def store_out(c, par):
                act.wait_ge(final_done, c + 1)
                act.dma_start(columns(outT, c), out_buf[par][:, :]).then_inc(out_stored[par], 16)

            def high(s, c, k):
                n = ph2_before(s, c, k)
                slot = k % R_RING
                a = a_tile(k % A_RING)
                act.wait_ge(a_loaded[k % A_RING],
                            16 * (PH1 // A_RING + 1 + k // A_RING)
                            + (16 // A_RING) * (PH2_BASE[s] + (c - GROUP * s) * PH2_N[s]))
                act.wait_ge(s_used, PH1 + n - R_RING + 1)
                if k % 2:
                    act.activation(tile(square_ring, slot), a, ACT.Square).then_inc(act_square, 1)
                act.activation(tile(high_ring, slot), a, ACT.Square).then_inc(high_ready, 1)

            def pair(s, c0):
                for par in range(2):
                    c = c0 + par
                    for k in range(PH2_N[s]):
                        high(s, c, k)
                        if k == 3 and not (isinstance(c, int) and c == 0):
                            store_out(c - 1, 1 - par)
                            if not (isinstance(c, int) and (c == NC - 1 or c == 1)):
                                load_acc(c + 1, 1 - par, c)
                        if isinstance(c, int) and c == 0:
                            if k == 5:
                                rstd(2 * NC - 1, 0, 0, False)
                            if k == NC - 1:
                                act.wait_ge(normed, 2 * NC)
                                load_acc(0, 0, None)
                                load_acc(1, 1, None)
                        if isinstance(c, int) and c == 1 and k == 5:
                            load_acc(2, 0, 1)

            phase2_pairs(act, pair, last_apart=True)
            store_out(NC - 1, 1)
            for par in range(2):
                act.wait_ge(out_stored[par], 16 * (NC // 2))

        @block.gpsimd
        def _(pool):
            pool.wait_ge(strip_zeroed, 1)
            eye = eye_strip[:, (GROUP - 1) * P:GROUP * P]
            pool.affine_select(out=eye, in_=eye, compare_op=ALU.not_equal, fill=1.0, base=0,
                               pattern=[[-1, P]], channel_multiplier=1).then_inc(strip_ready, 1)

            def square_deviation(n, b, cb, apart):
                pool.wait_ge(centred, n + 1)
                if not (isinstance(n, int) and n < 2):
                    pool.wait_ge(var_done, n - 1 if apart else n)
                pool.tensor_tensor(square_buf[b][:, :], centred_buf[cb][:, :], centred_buf[cb][:, :],
                                   ALU.mult).then_inc(dev_squared, 1)

            for n in range(NC):
                square_deviation(n, n % 2, n % 3, True)

            def square_adj(s, c, i):
                n, r = l2_before(s, c, i), L2_RANK[s][i]
                pool.wait_ge(a_loaded[i % A_RING], 16 * (c * (NC // A_RING) + i // A_RING + 1))
                if not (isinstance(n, int) and n < Q_RING):
                    pool.wait_ge(q_used, n - Q_RING + 1)
                a = a_tile(i % A_RING)
                pool.tensor_tensor(tile(q_ring, r % Q_RING), a, a, ALU.mult).then_inc(q_ready, 1)

            def chunk(s, c):
                for i in range(NC):
                    if i == 6:
                        square_deviation(c + NC - 1, 0, 0, False)
                    if ORDER[s][i] < GROUP * s:
                        square_adj(s, c, i)

            phase1_chunks(pool, chunk)

            def pair(s, c0):
                for par in range(2):
                    c = c0 + par
                    for k in range(0, PH2_N[s], 2):
                        n = ph2_before(s, c, k)
                        pool.wait_ge(a_loaded[k % A_RING],
                                     16 * (PH1 // A_RING + 1 + k // A_RING)
                                     + (16 // A_RING) * (PH2_BASE[s] + (c - GROUP * s) * PH2_N[s]))
                        pool.wait_ge(s_used, PH1 + n - R_RING + 1)
                        a = a_tile(k % A_RING)
                        pool.tensor_tensor(tile(square_ring, k % R_RING), a, a,
                                           ALU.mult).then_inc(pool_square, 1)
                        if isinstance(c, int) and c == 0 and k == 0:
                            square_deviation(2 * NC - 1, 0, 0, False)

            phase2_pairs(pool, pair)


def kernel(x, adj, L0_gnn_W, L0_gnn_B, L0_gnn_mu, L0_gnn_sigma, L1_gnn_W):
    import numpy as np
    import concourse.bacc as bacc
    from concourse.bass_utils import run_bass_kernel_spmd

    tiles = np.asarray(adj).reshape(NC, CHUNK, NC, G, P).transpose(0, 2, 4, 3, 1)
    arrays = {
        "xT": np.ascontiguousarray(np.asarray(x).T),
        "adjT": np.ascontiguousarray(tiles).reshape(NC * NC, P, TILE),
        "W0": np.ascontiguousarray(L0_gnn_W),
        "B0": np.ascontiguousarray(L0_gnn_B),
        "mu": np.ascontiguousarray(L0_gnn_mu),
        "sigma": np.ascontiguousarray(L0_gnn_sigma),
        "W1T": np.ascontiguousarray(np.asarray(L1_gnn_W).T),
    }
    nc = bacc.Bacc("TRN2", target_bir_lowering=False, num_devices=1)
    args = [nc.dram_tensor(name, a.shape, mybir.dt.from_np(a.dtype), kind="ExternalInput").ap()
            for name, a in arrays.items()]
    outT = nc.dram_tensor("outT", (D, N), F32, kind="ExternalOutput").ap()
    gnn_program(nc, *args, outT)
    r = run_bass_kernel_spmd(nc, [arrays], core_ids=[0])
    return np.ascontiguousarray(r.results[0]["outT"].T)
```

```python
from contextlib import ExitStack

import concourse.bass as bass
from concourse import mybir

ALU = mybir.AluOpType
ACT = mybir.ActivationFunctionType
F32 = mybir.dt.float32
F32R = mybir.dt.float32r

P = 128
D = 128
N = 8192
CHUNK = 512
NC = N // CHUNK
G = CHUNK // P
TILE = G * CHUNK
GROUP = 4
NG = NC // GROUP
A_RING = 4
S_RING = 8
Q_RING = 2
R_RING = 4
DIAG = CHUNK + P
LN_EPS = 1e-5
CUTOFF = 0.5
TINY = 2.0 ** -60

L2_STEPS = [(), (3, 7, 11, 15), (1, 4, 5, 8, 9, 12, 13, 15), (1, 2, 3, 5, 6, 7, 9, 10, 11, 13, 14, 15)]


def order_of(s):
    with_l2, without = iter(range(GROUP * s)), iter(range(GROUP * s, NC))
    return [next(with_l2) if i in L2_STEPS[s] else next(without) for i in range(NC)]


ORDER = [order_of(s) for s in range(NG)]
HALF = NC // 2
DVE_ADD_REST, DVE_CENTRE, DVE_NORM, DVE_KEEP, DVE_COMPLETE, DVE_ADD_HALF = 4, 7, 11, 13, 15, 12
PE_MEAN, PE_VARIANCE, PE_PROJECT = 2, 5, 8
POOL_SQUARE, ACT_RSTD = 7, 10
WHOLE, FIRST_HALF, SECOND_HALF = range(G), range(G // 2), range(G // 2, G)
EXTRAS = {1: [(J, WHOLE) for J in range(GROUP)],
          2: [(J, half) for J in (GROUP, GROUP + 1) for half in (FIRST_HALF, SECOND_HALF)]}
EXTRA_AFTER = (2, 6, 10, 14)


def items_of(s):
    items = []
    for i, J in enumerate(ORDER[s]):
        items.append((J, WHOLE, i))
        if s in EXTRAS and i in EXTRA_AFTER:
            items.append((*EXTRAS[s][EXTRA_AFTER.index(i)], None))
    return items


ITEMS = [items_of(s) for s in range(NG)]
LOADS = [len(items) for items in ITEMS]
LOAD_BASE = [GROUP * sum(LOADS[:s]) for s in range(NG + 1)]
PLACE = [[items.index((J, WHOLE, i)) for i, J in enumerate(ORDER[s])] for s, items in enumerate(ITEMS)]
OWN_RANK = [[sum(i is not None for *_, i in items[:p]) for p in range(len(items) + 1)]
            for items in ITEMS]
L2_RANK = [[sum(i is None or J < GROUP * s for J, _, i in items[:p]) for p in range(len(items) + 1)]
           for s, items in enumerate(ITEMS)]
LEAD, L2_FROM = 1, 1


def l2_loads_at(s, i):
    def step(p):
        return max(n for *_, n in ITEMS[s][:p + 1] if n is not None)

    return [p for p, (J, _, n) in enumerate(ITEMS[s])
            if (n is None or J < GROUP * s) and i == min(max(step(p) - LEAD, L2_FROM), NC - 1)]


L2_N = [ranks[-1] for ranks in L2_RANK]
L2_BASE = [GROUP * sum(L2_N[:s]) for s in range(NG + 1)]
PH1 = NC * NC
PH2_FIRST = [GROUP * s for s in range(NG)]
for s, extras in EXTRAS.items():
    PH2_FIRST[s - 1] = extras[-1][0] + 1
PH2_N = [NC - first for first in PH2_FIRST]
PH2_BASE = [GROUP * sum(PH2_N[:s]) for s in range(NG)]


def l2_before(s, c, p):
    return L2_BASE[s] + (c - GROUP * s) * L2_N[s] + L2_RANK[s][p]


def load_rounds(s, c, p):
    return LOAD_BASE[s] // A_RING + (c - GROUP * s) * (LOADS[s] // A_RING) + p // A_RING + 1


def group_before(s, c):
    return (c - 1) // GROUP if isinstance(c, int) else s


def loads_back(s, c, p, back):
    if p >= back:
        return s, c, p - back
    before = group_before(s, c)
    return before, c - 1, p - back + LOADS[before]


def ph2_before(s, c0, j):
    return PH2_BASE[s] + (c0 - GROUP * s) * PH2_N[s] + j


def ph2_half(s, c0, j):
    return PH2_BASE[s] // 2 + (c0 - GROUP * s) * (PH2_N[s] // 2) + j // 2


def ph2_loaded(s, c0, j):
    return (16 * (LOAD_BASE[NG] // A_RING + 1 + j // A_RING)
            + (16 // A_RING) * (PH2_BASE[s] + (c0 - GROUP * s) * PH2_N[s]))


def phase1_chunks(eng, body):
    for s in range(NG):
        first = max(1, GROUP * s)
        body(s, first)
        with eng.Fori(first + 1, GROUP * (s + 1)) as c:
            body(s, c)


def phase2_pairs(eng, body, first_apart=False, last_apart=False):
    for s in range(NG):
        lo, hi = GROUP * s, GROUP * (s + 1)
        if s == 0 or first_apart or (s == NG - 1 and last_apart):
            for c in range(lo, hi, 2):
                body(s, c)
        else:
            with eng.Fori(lo // 2, hi // 2) as half:
                body(s, half * 2)


def gnn_program(nc, xT, adjT, W0, B0, mu, sigma, W1T, outT):
    with ExitStack() as ctx:
        def sb(name, shape):
            return ctx.enter_context(nc.sbuf_tensor(name, shape, F32))

        def bank(name):
            return ctx.enter_context(nc.psum_tensor(name, [P, CHUNK], F32))

        def sem(name):
            return ctx.enter_context(nc.semaphore(name))

        acc_dram = nc.dram_tensor("acc_dram", [D, N], F32).ap()

        h_size, s_size, q_size = NC * G * D, S_RING * TILE, Q_RING * TILE
        arena_size = 4 * (2 * h_size + s_size + q_size)
        ctx.enter_context(nc.sbuf_tensor("arena", [P, arena_size // 4], F32))
        arena = nc.sbuf_base - arena_size

        def at(name, shape, words, dtype=F32):
            return nc.alloc_sbuf_tensor_at(name, shape, dtype, offset=arena + 4 * words)

        h1 = at("h1", [P, NC * G, D], 0)
        h2 = at("h2", [P, NC * G, D], h_size)
        s_ring = at("s_ring", [P, s_size], 2 * h_size)
        q_ring = at("q_ring", [P, q_size], 2 * h_size + s_size)
        h2_high = at("h2_high", [P, NC * G, D], 0, F32R)
        h2_low = at("h2_low", [P, NC * G, D], h_size, F32R)
        high_ring = at("high_ring", [P, R_RING * TILE], 2 * h_size, F32R)
        low_ring = at("low_ring", [P, R_RING * TILE], 2 * h_size + R_RING * TILE, F32R)
        square_ring = at("square_ring", [P, R_RING * TILE], 2 * h_size + R_RING * TILE)

        a_ring = sb("a_ring", [P, A_RING * TILE + CHUNK])
        x_buf = [sb(f"x_buf{n}", [D, CHUNK]) for n in range(2)]
        centred_buf = [sb(f"centred_buf{n}", [D, CHUNK]) for n in range(3)]
        square_buf = [sb(f"square_buf{n}", [D, CHUNK]) for n in range(2)]
        rstd_buf = [sb(f"rstd_buf{n}", [D, CHUNK]) for n in range(2)]
        normed_buf = [sb(f"normed_buf{n}", [D, CHUNK]) for n in range(2)]
        acc_buf = square_buf[1]
        extra_buf = x_buf[1]
        rstd_columns = rstd_buf[1]
        acc_in = rstd_buf
        out_buf = normed_buf
        bias_rows = sb("bias_rows", [P, D])
        w0 = sb("w0", [D, D])
        w1 = sb("w1", [D, D])
        mean_of = sb("mean_of", [D, D])
        eye_strip = sb("eye_strip", [P, (2 * GROUP - 1) * P])
        small = sb("small", [P, 16])
        mu_c, sigma_c, inv_mu, neg_2c, var2, inv_var2, neg_k, c_sq, exp_bias, tiny_c, eps_c = (
            small[:, n:n + 1] for n in range(11))

        p_l1 = bank("p_l1")
        p_l2 = [bank("p_l2a"), bank("p_l2b")]
        p_stat = [bank("p_stat0"), bank("p_stat1"), bank("p_stat2"), p_l2[1]]
        p_rest = p_stat[1]
        p_proj = [bank("p_proj0"), bank("p_proj1")]

        a_loaded = [sem(f"a_loaded{n}") for n in range(A_RING)]
        x_loaded = [sem("x_loaded0"), sem("x_loaded1")]
        weights_loaded = sem("weights_loaded")
        params_loaded = sem("params_loaded")
        param_step = sem("param_step")
        strip_zeroed = sem("strip_zeroed")
        strip_ready = sem("strip_ready")
        diag_marked = sem("diag_marked")
        premasked = sem("premasked")
        ln_done = sem("ln_done")
        recip_done = sem("recip_done")
        squared = sem("squared")
        sens_done = sem("sens_done")
        s_used = sem("s_used")
        q_ready = sem("q_ready")
        q_used = sem("q_used")
        half_added = sem("half_added")
        x1_added = sem("x1_added")
        acc_added = sem("acc_added")
        acc_complete = sem("acc_complete")
        acc_stored = sem("acc_stored")
        extra_loaded = sem("extra_loaded")
        extra_added = sem("extra_added")
        extra_stored = sem("extra_stored")
        mean_done = sem("mean_done")
        centred = sem("centred")
        dev_squared = sem("dev_squared")
        var_done = sem("var_done")
        log_var_done = sem("log_var_done")
        rstd_done = sem("rstd_done")
        normed = sem("normed")
        projected = sem("projected")
        h_ready = sem("h_ready")
        h_split = sem("h_split")
        h_high_done = sem("h_high_done")
        high_ready = sem("high_ready")
        pool_square = sem("pool_square")
        low_ready = sem("low_ready")
        final_done = sem("final_done")
        acc_loaded = [sem("acc_loaded0"), sem("acc_loaded1")]
        out_stored = [sem("out_stored0"), sem("out_stored1")]

        def tile(ring, slot):
            return ring[:, slot * TILE:(slot + 1) * TILE]

        def a_tile(slot):
            return tile(a_ring, slot)

        def s_tile(slot):
            return tile(s_ring, slot)

        def diagonal(ring, slot):
            v = ring[:, slot * TILE:slot * TILE + G * DIAG]
            return v.rearrange("p (g n) -> p g n", g=G)[:, :, 0:P]

        def eye_if_diagonal(J, c, s):
            first = c * P + (GROUP - 1 - J) * P
            return eye_strip[:, bass.ds(first, P)].unsqueeze(1).to_broadcast([P, G, P])

        def blocks_of(ring, slot, blocks):
            start = slot * TILE + blocks[0] * CHUNK
            return ring[:, start:start + len(blocks) * CHUNK]

        def adj_tile(c, J, blocks=WHOLE):
            v = adjT[bass.ds(c * NC + J, 1), :, :].rearrange("t p n -> p (t n)")
            return v[:, blocks[0] * CHUNK:(blocks[-1] + 1) * CHUNK]

        def columns(dram, c):
            return dram[:, bass.ds(c * CHUNK, CHUNK)]

        block = ctx.enter_context(nc.Block())

        @block.sync
        def _(sp):
            def free_slot(s, c, p):
                s, c, p = loads_back(s, c, p, A_RING)
                squares = l2_before(s, c, p + 1)
                if not isinstance(squares, int):
                    sp.compute_val(squares)
                sp.wait_ge(premasked, c * NC + OWN_RANK[s][p + 1])
                if not (isinstance(squares, int) and squares == 0):
                    sp.wait_ge(q_ready, squares)

            def load_tile(s, c, p):
                J, blocks, i = ITEMS[s][p]
                if not (isinstance(c, int) and c == 0 and p < A_RING):
                    free_slot(s, c, p)
                target = c if i is not None else c - GROUP
                sp.dma_start(blocks_of(a_ring, p % A_RING, blocks),
                             adj_tile(target, J, blocks)).then_inc(a_loaded[p % A_RING], 16)

            def load_x(n):
                if n >= 2:
                    sp.wait_ge(centred, n - 1)
                sp.dma_start(x_buf[n % 2][:, :], columns(xT, n)).then_inc(x_loaded[n % 2], 16)

            load_tile(0, 0, 0)
            load_x(0)
            load_tile(0, 0, 1)
            load_x(1)
            sp.dma_start(mu_c, mu.partition_broadcast(P)).then_inc(params_loaded, 16)
            sp.dma_start(sigma_c, sigma.partition_broadcast(P)).then_inc(params_loaded, 16)
            sp.dma_start(w0[:, :], W0).then_inc(weights_loaded, 16)
            sp.dma_start(w1[:, :], W1T).then_inc(weights_loaded, 16)
            sp.dma_start(bias_rows[:, :], B0.partition_broadcast(P)).then_inc(weights_loaded, 16)
            for i in range(2, NC):
                load_tile(0, 0, i)
                load_x(i)

            def load_residual(c):
                sp.wait_ge(centred, c + NC)
                sp.dma_start(x_buf[0][:, :], columns(xT, c)).then_inc(x_loaded[0], 16)

            def store_acc(c):
                sp.wait_ge(acc_complete, c + 1)
                sp.dma_start(columns(acc_dram, c), acc_buf[:, :]).then_inc(acc_stored, 16)

            def chunk(s, c):
                for p in range(LOADS[s]):
                    load_tile(s, c, p)
                    i = ITEMS[s][p][-1]
                    if i == 4 and not (isinstance(c, int) and c == 1):
                        store_acc(c - 2)
                    if i == 3 and isinstance(c, int) and c == 1:
                        load_residual(0)
                    if i == 11:
                        load_residual(c)
                    if i == 9 and group_before(s, c) in EXTRAS:
                        sp.wait_ge(extra_added, c - GROUP)
                        sp.dma_start(columns(acc_dram, c - 1 - GROUP), extra_buf[:, :]).then_inc(
                            extra_stored, 16)
                    if i == 12 and s in EXTRAS:
                        sp.wait_ge(acc_stored, 16 * (c - GROUP + 1))
                        if not (isinstance(c, int) and c == GROUP):
                            sp.wait_ge(extra_stored, 16 * (c - GROUP))
                        sp.dma_start(extra_buf[:, :], columns(acc_dram, c - GROUP)).then_inc(
                            extra_loaded, 16)

            phase1_chunks(sp, chunk)
            store_acc(NC - 2)

            def load_tile2(s, c0, j):
                n = ph2_before(s, c0, j)
                if isinstance(n, int) and n < A_RING:
                    free_slot(NG - 1, NC - 1, LOADS[NG - 1] + n)
                else:
                    if j % 2 == 0:
                        pool_squares = ph2_half(s, c0, j) - A_RING // 2 + 1
                        if not isinstance(n, int):
                            sp.compute_val(pool_squares)
                    sp.wait_ge(high_ready, n - A_RING + 1)
                    if j % 2 == 0:
                        sp.wait_ge(pool_square, pool_squares)
                par, k = divmod(j, PH2_N[s])
                sp.dma_start(a_tile(j % A_RING), adj_tile(c0 + par, PH2_FIRST[s] + k)).then_inc(
                    a_loaded[j % A_RING], 16)

            def pair(s, c0):
                for j in range(2 * PH2_N[s]):
                    load_tile2(s, c0, j)
                    if isinstance(c0, int) and c0 == 0 and j == PH2_N[s]:
                        store_acc(NC - 1)

            phase2_pairs(sp, pair)

        @block.tensor
        def _(pe):
            def l1(s, c, i):
                J, t = ORDER[s][i], c * NC + i
                if isinstance(c, int) and c == 0:
                    pe.wait_ge(h_ready, J + 1)
                elif i == 0 and isinstance(c, int) and c == 1:
                    pe.wait_ge(x1_added, 1)
                elif i == 0:
                    pe.wait_ge(half_added, c - 1)
                elif i == HALF:
                    pe.wait_ge(x1_added, c)
                whole = isinstance(c, int) and c == 0
                out = p_l1 if whole or i < HALF else p_rest
                pe.wait_ge(sens_done, t + 1)
                for g in range(G):
                    last = pe.matmul(out[:, :], h1[:, J * G + g, :],
                                     s_tile(i % S_RING)[:, g * CHUNK:(g + 1) * CHUNK],
                                     start=((i == 0 or (i == HALF and not whole)) and g == 0),
                                     stop=((i == NC - 1 or (i == HALF - 1 and not whole))
                                           and g == G - 1))
                last.then_inc(s_used, 1)

            def l2(s, c, p):
                (J, blocks, i), r = ITEMS[s][p], L2_RANK[s][p]
                extra = i is None
                first = (J, blocks) == (EXTRAS[s][0] if extra else (0, WHOLE))
                final = (J, blocks) == (EXTRAS[s][-1] if extra else (GROUP * s - 1, WHOLE))
                if first and not extra:
                    pe.wait_ge(acc_added, c)
                if first and extra and not (isinstance(c, int) and c == GROUP):
                    pe.wait_ge(extra_added, c - GROUP)
                pe.wait_ge(h_ready, NC + J + 1)
                pe.wait_ge(q_ready, l2_before(s, c, p) + 1)
                for g in blocks:
                    last = pe.matmul(p_l2[1 if extra else 0][:, :], h2[:, J * G + g, :],
                                     tile(q_ring, r % Q_RING)[:, g * CHUNK:(g + 1) * CHUNK],
                                     start=(first and g == blocks[0]),
                                     stop=(final and g == blocks[-1]))
                last.then_inc(q_used, 1)

            def mean(n, b):
                if b is None:
                    pe.wait_ge(rstd_done, n)
                    pe.wait_ge(x1_added, n - NC + 1)
                elif n >= 4:
                    pe.wait_ge(rstd_done, n - 3)
                if b is not None:
                    pe.wait_ge(x_loaded[b], 16 * (n // 2 + 1))
                sb_ = 0 if b is None else n % 4
                b = b or 0
                pe.matmul(p_stat[sb_][:, :], mean_of[:, :], x_buf[b][:, :], start=True,
                          stop=True).then_inc(mean_done, 1)

            def node_variances(n, b, stat):
                pe.wait_ge(dev_squared, n + 1)
                for g in range(G):
                    last = pe.matmul(p_stat[stat][:, g:g + 1], square_buf[b][:, g * P:(g + 1) * P],
                                     mean_of[:, 0:1], start=True, stop=True)
                last.then_inc(var_done, 1)

            def variance(n, b, stat):
                pe.wait_ge(dev_squared, n + 1)
                pe.matmul(p_stat[stat][:, :], mean_of[:, :], square_buf[b][:, :], start=True,
                          stop=True).then_inc(var_done, 1)

            def project(n, b, w, apart):
                pe.wait_ge(normed, n + 1)
                if not apart:
                    if not (isinstance(n, int) and n == NC):
                        pe.wait_ge(acc_complete, n - NC)
                    pe.matmul(p_proj[1][:, :], w[:, :], normed_buf[b][:, :], start=True, stop=True)
                if not (isinstance(n, int) and n < 2):
                    pe.wait_ge(h_ready, n - 1 if apart else n)
                for g in range(G):
                    last = pe.matmul(p_proj[b][:, g * P:(g + 1) * P],
                                     normed_buf[b][:, g * P:(g + 1) * P], w[:, :],
                                     start=True, stop=True)
                last.then_inc(projected, 1)

            pe.wait_ge(param_step, 2)
            mean(0, 0)
            for m in range(NC + 3):
                if m + 1 < NC:
                    mean(m + 1, (m + 1) % 2)
                if m >= 5:
                    l1(0, 0, m - 5)
                if m < NC:
                    node_variances(m, m % 2, m % 4)
                if m == 2:
                    pe.wait_ge(weights_loaded, 48)
                if 2 <= m < NC + 2:
                    project(m - 2, m % 2, w0, True)
            for i in (NC - 2, NC - 1):
                l1(0, 0, i)

            def chunk(s, c):
                for i in range(NC):
                    l1(s, c, i)
                    if i == PE_MEAN:
                        mean(c + NC - 1, None)
                    for p in l2_loads_at(s, i):
                        l2(s, c, p)
                    if i == PE_VARIANCE:
                        variance(c + NC - 1, 0, 0)
                    if i == PE_PROJECT:
                        project(c + NC - 1, 0, w1, False)

            phase1_chunks(pe, chunk)

            def l2_rest(s, c0, j):
                par, k = divmod(j, PH2_N[s])
                J = PH2_FIRST[s] + k
                if isinstance(c0, int) and c0 == 0 and par == 0:
                    pe.wait_ge(h_split, k + 1)
                pe.wait_ge(low_ready, ph2_before(s, c0, j) + 1)
                for g in range(G):
                    columns_of_g = slice(j % R_RING * TILE + g * CHUNK,
                                         j % R_RING * TILE + (g + 1) * CHUNK)
                    high, low = high_ring[:, columns_of_g], low_ring[:, columns_of_g]
                    parts = ((h2_high, high), (h2_high, low), (h2_low, high))
                    for m, (h, q) in enumerate(parts):
                        last = pe.matmul(p_l2[1 - par][:, :], h[:, J * G + g, :], q,
                                         start=(k == 0 and g == 0 and m == 0),
                                         stop=(k == PH2_N[s] - 1 and g == G - 1
                                               and m == len(parts) - 1))
                last.then_inc(s_used, 1)

            def pair(s, c0):
                for j in range(2 * PH2_N[s]):
                    par, k = divmod(j, PH2_N[s])
                    c = c0 + par
                    if k == 0 and isinstance(c, int) and c == 1:
                        pe.wait_ge(acc_added, NC)
                    elif k == 0 and not (isinstance(c, int) and c == 0):
                        pe.wait_ge(final_done, c - 1)
                    l2_rest(s, c0, j)
                    if isinstance(c, int) and c == 0:
                        if k == 0:
                            mean(2 * NC - 1, None)
                        if k == 2:
                            variance(2 * NC - 1, 0, 0)
                        if k == 5:
                            project(2 * NC - 1, 0, w1, False)

            phase2_pairs(pe, pair)

        @block.vector
        def _(dve):
            steps = [0]

            def small_step(instruction):
                steps[0] += 1
                instruction.then_inc(param_step, 1)
                dve.wait_ge(param_step, steps[0])

            dve.memset(eye_strip[:, :], 0.0).then_inc(strip_zeroed, 1)
            small_step(dve.memset(tiny_c, TINY))
            small_step(dve.memset(mean_of[:, :], 1.0 / D))
            small_step(dve.memset(eps_c, LN_EPS))
            dve.wait_ge(strip_ready, 1)

            def constants():
                dve.wait_ge(params_loaded, 32)
                small_step(dve.reciprocal(inv_mu, mu_c))
                small_step(dve.tensor_scalar(neg_2c, inv_mu, -2.0, None, ALU.mult))
                small_step(dve.tensor_tensor(var2, sigma_c, sigma_c, ALU.mult))
                small_step(dve.tensor_scalar(var2, var2, 2.0, None, ALU.mult))
                small_step(dve.reciprocal(inv_var2, var2))
                small_step(dve.tensor_scalar(neg_k, inv_var2, -1.0, None, ALU.mult))
                small_step(dve.tensor_tensor(c_sq, inv_mu, inv_mu, ALU.mult))
                small_step(dve.tensor_tensor(exp_bias, c_sq, neg_k, ALU.mult))

            def premask(s, c, i):
                J, t = ORDER[s][i], c * NC + i
                slot = PLACE[s][i] % A_RING
                dve.wait_ge(a_loaded[slot], 16 * load_rounds(s, c, PLACE[s][i]))
                if GROUP * s <= J < GROUP * (s + 1):
                    d = diagonal(a_ring, slot)
                    dve.tensor_tensor(d, d, eye_if_diagonal(J, c, s), ALU.add).then_inc(diag_marked, 1)
                    dve.wait_ge(diag_marked, c * GROUP + J - GROUP * s + 1)
                if not (isinstance(c, int) and t < S_RING):
                    dve.wait_ge(s_used, t - S_RING + 1)
                dve.scalar_tensor_tensor(out=s_tile(i % S_RING), in0=a_tile(slot), scalar=CUTOFF,
                                         in1=a_tile(slot), op0=ALU.is_lt,
                                         op1=ALU.mult).then_inc(premasked, 1)

            def square(t, slot):
                dve.wait_ge(recip_done, t + 1)
                v = s_tile(slot)
                dve.scalar_tensor_tensor(out=v, in0=v, scalar=neg_2c, in1=v, op0=ALU.add,
                                         op1=ALU.mult).then_inc(squared, 1)

            def centre(n, b, cb, stat):
                if isinstance(n, int) and 3 <= n < NC:
                    dve.wait_ge(normed, n - 2)
                dve.wait_ge(mean_done, n + 1)
                dve.tensor_tensor(centred_buf[cb][:, :], x_buf[b][:, :], p_stat[stat][:, :],
                                  ALU.subtract).then_inc(centred, 1)

            def norm_relu(n):
                dve.wait_ge(rstd_done, n + 1)
                dve.wait_ge(projected, n)
                dve.scalar_tensor_tensor(out=normed_buf[0][:, :], in0=centred_buf[0][:, :], scalar=0.0,
                                         in1=rstd_buf[0][:, :], op0=ALU.max,
                                         op1=ALU.mult).then_inc(normed, 1)

            def keep_h1(n):
                dve.wait_ge(projected, n + 1)
                dve.wait_ge(rstd_done, n + 1)
                if n == 0:
                    dve.wait_ge(weights_loaded, 48)
                for g in range(G):
                    block_n = n * G + g
                    last = dve.scalar_tensor_tensor(
                        out=h1[:, block_n, :], in0=p_proj[n % 2][:, g * P:(g + 1) * P],
                        scalar=rstd_columns[:, block_n:block_n + 1], in1=bias_rows[:, :],
                        op0=ALU.mult, op1=ALU.add)
                last.then_inc(h_ready, 1)

            def complete_acc(c):
                dve.wait_ge(projected, c + NC + 1)
                dve.wait_ge(acc_added, c + 1)
                dve.tensor_tensor(acc_buf[:, :], p_proj[1][:, :], acc_buf[:, :],
                                  ALU.add).then_inc(acc_complete, 1)

            def keep_h2(c):
                dve.wait_ge(projected, c + NC + 1)
                dve.tensor_copy(h2[:, bass.ds(c * G, G), :],
                                p_proj[0][:, :].rearrange("p (g n) -> p g n", g=G)).then_inc(h_ready, 1)

            def add_half(c):
                dve.wait_ge(s_used, c * NC + HALF)
                dve.wait_ge(x_loaded[0], 16 * (c + NC // 2 + 1))
                dve.tensor_tensor(x_buf[0][:, :], p_l1[:, :], x_buf[0][:, :],
                                  ALU.add).then_inc(half_added, 1)

            def add_x1(c):
                dve.wait_ge(s_used, (c + 1) * NC)
                if isinstance(c, int) and c == 0:
                    dve.wait_ge(x_loaded[0], 16 * (NC // 2 + 1))
                else:
                    dve.wait_ge(half_added, c)
                rest = p_l1 if isinstance(c, int) and c == 0 else p_rest
                dve.tensor_tensor(x_buf[0][:, :], rest[:, :], x_buf[0][:, :],
                                  ALU.add).then_inc(x1_added, 1)

            def add_extra(l2_tiles, c):
                dve.wait_ge(q_used, l2_tiles)
                dve.wait_ge(extra_loaded, 16 * (c + 1))
                dve.tensor_tensor(extra_buf[:, :], p_l2[1][:, :], extra_buf[:, :],
                                  ALU.add).then_inc(extra_added, 1)

            def add_acc(s, c, l2_tiles):
                dve.wait_ge(x1_added, c + 1)
                if not (isinstance(c, int) and c == 0):
                    dve.wait_ge(acc_stored, 16 * c)
                if s == 0:
                    dve.tensor_copy(acc_buf[:, :], x_buf[0][:, :]).then_inc(acc_added, 1)
                else:
                    dve.wait_ge(q_used, l2_tiles)
                    dve.tensor_tensor(acc_buf[:, :], p_l2[0][:, :], x_buf[0][:, :],
                                      ALU.add).then_inc(acc_added, 1)

            for i in range(NC):
                premask(0, 0, i)
                centre(i, i % 2, i % 3, i % 4)
                if i == 1:
                    constants()
                if i >= 2:
                    square(i - 2, (i - 2) % S_RING)
                if i >= 4:
                    keep_h1(i - 4)
            keep_h1(NC - 4)

            def chunk(s, c):
                before = group_before(s, c)
                for i in range(NC):
                    premask(s, c, i)
                    if isinstance(c, int) and c == 1 and i < 3:
                        keep_h1(NC - 3 + i)
                    square(c * NC + i - 2, (i - 2) % S_RING)
                    if i == DVE_ADD_REST:
                        if before in EXTRAS:
                            add_extra(l2_before(s, c, 0), c - 1 - GROUP)
                        add_x1(c - 1)
                        add_acc(before, c - 1, l2_before(s, c, 0))
                    if i == DVE_CENTRE:
                        centre(c + NC - 1, 0, 0, 0)
                    if i == DVE_NORM:
                        norm_relu(c + NC - 1)
                    if i == DVE_ADD_HALF:
                        add_half(c)
                    if i == DVE_KEEP:
                        keep_h2(c - 1)
                    if i == DVE_COMPLETE:
                        complete_acc(c - 1)

            phase1_chunks(dve, chunk)
            square(PH1 - 2, (NC - 2) % S_RING)
            square(PH1 - 1, (NC - 1) % S_RING)

            def split_h2(J):
                at_step = ORDER[NG - 1].index(J)
                dve.wait_ge(s_used, PH1 - NC + at_step + 1)
                if J < GROUP * (NG - 1):
                    dve.wait_ge(q_used, l2_before(NG - 1, NC - 1, PLACE[NG - 1][at_step] + 1))
                if J == NC - 1:
                    dve.wait_ge(h_ready, 2 * NC)
                rows = slice(J * G, (J + 1) * G)
                dve.tensor_copy(h2_high[:, rows, :], h2[:, rows, :]).then_inc(h_high_done, 1)
                dve.wait_ge(h_high_done, J - PH2_FIRST[0] + 1)
                dve.tensor_tensor(h2_low[:, rows, :], h2[:, rows, :],
                                  h2_high[:, rows, :].bitcast(F32), ALU.subtract).then_inc(h_split, 1)

            def low(s, c0, j):
                dve.wait_ge(high_ready, ph2_before(s, c0, j) + 1)
                if j % 2 == 0:
                    dve.wait_ge(pool_square, ph2_half(s, c0, j) + 1)
                slot = j % R_RING
                dve.tensor_tensor(tile(low_ring, slot), tile(square_ring, slot),
                                  tile(high_ring, slot).bitcast(F32), ALU.subtract).then_inc(low_ready, 1)

            def finish(tiles, par, stored):
                dve.wait_ge(s_used, PH1 + tiles)
                dve.wait_ge(acc_loaded[par], stored + 16)
                if not (isinstance(stored, int) and stored == 0):
                    dve.wait_ge(out_stored[par], stored)
                dve.tensor_tensor(out_buf[par][:, :], p_l2[1 - par][:, :], acc_in[par][:, :],
                                  ALU.add).then_inc(final_done, 1)

            def pair(s, c0):
                for j in range(2 * PH2_N[s]):
                    par, k = divmod(j, PH2_N[s])
                    if not (isinstance(c0, int) and c0 == 0 and j < 2):
                        low(s, c0, j)
                    if k == 2 and not (isinstance(c0, int) and c0 + par == 0):
                        finish(ph2_before(s, c0, j - k), 1 - par, 8 * (c0 - 2) + 16 * par)
                    if isinstance(c0, int) and c0 + par == 0:
                        last_job(k)

            def last_job(k):
                if k == 2:
                    split_h2(11)
                    split_h2(12)
                if k == 3:
                    split_h2(13)
                    split_h2(14)
                if k == 4:
                    norm_relu(2 * NC - 1)
                if k == 7:
                    keep_h2(NC - 1)
                    split_h2(NC - 1)
                    complete_acc(NC - 1)

            for J in (4, 5, 6, 7):
                split_h2(J)
            low(0, 0, 0)
            for J in (8, 9, 10):
                split_h2(J)
            low(0, 0, 1)
            add_x1(NC - 1)
            centre(2 * NC - 1, 0, 0, 0)
            add_acc(NG - 1, NC - 1, L2_BASE[NG])
            phase2_pairs(dve, pair, first_apart=True)
            finish(ph2_before(NG - 1, NC, 0), 1, 16 * (NC // 2 - 1))

        @block.scalar
        def _(act):
            act.preload_act_table_set("natural_log_exp_and_others")
            act.wait_ge(param_step, 3)

            def log(c, i):
                act.wait_ge(premasked, c * NC + i + 1)
                v = s_tile(i % S_RING)
                act.activation(v, v, ACT.Ln, bias=tiny_c).then_inc(ln_done, 1)

            def reciprocal(t, slot):
                act.wait_ge(ln_done, t + 1)
                v = s_tile(slot)
                act.activation(v, v, ACT.Exp, scale=-1.0).then_inc(recip_done, 1)

            def sensitivity(t, slot):
                act.wait_ge(squared, t + 1)
                v = s_tile(slot)
                act.activation(v, v, ACT.Exp, bias=exp_bias, scale=neg_k).then_inc(sens_done, 1)

            def rstd(n, out, variances):
                act.wait_ge(var_done, n + 1)
                act.activation(out, variances, ACT.Ln, bias=eps_c).then_inc(log_var_done, 1)
                act.wait_ge(log_var_done, n + 1)
                act.activation(out, out, ACT.Exp, scale=-0.5).then_inc(rstd_done, 1)

            def node_rstd(n):
                rstd(n, rstd_columns[:, n * G:(n + 1) * G], p_stat[n % 4][:, 0:G])

            def row_rstd(n):
                act.wait_ge(normed, n)
                rstd(n, rstd_buf[0][:, :], p_stat[0][:, :])

            for i in range(NC):
                log(0, i)
                if i >= 1:
                    reciprocal(i - 1, (i - 1) % S_RING)
                    node_rstd(i - 1)
                if i == 2:
                    act.wait_ge(param_step, 11)
                if i >= 2:
                    sensitivity(i - 2, (i - 2) % S_RING)
            node_rstd(NC - 1)

            def chunk(s, c):
                for i in range(NC):
                    log(c, i)
                    reciprocal(c * NC + i - 1, (i - 1) % S_RING)
                    sensitivity(c * NC + i - 2, (i - 2) % S_RING)
                    if i == ACT_RSTD:
                        row_rstd(c + NC - 1)

            phase1_chunks(act, chunk)
            reciprocal(PH1 - 1, (NC - 1) % S_RING)
            sensitivity(PH1 - 2, (NC - 2) % S_RING)
            sensitivity(PH1 - 1, (NC - 1) % S_RING)

            def load_acc(c, par, finished):
                act.wait_ge(acc_stored, 16 * (c + 1))
                if isinstance(c, int) and c == 0:
                    act.wait_ge(extra_stored, 16 * GROUP * len(EXTRAS))
                if finished is not None:
                    act.wait_ge(final_done, finished)
                act.dma_start(acc_in[par][:, :], columns(acc_dram, c)).then_inc(acc_loaded[par], 16)

            def store_out(c, par):
                act.wait_ge(final_done, c + 1)
                act.dma_start(columns(outT, c), out_buf[par][:, :]).then_inc(out_stored[par], 16)

            def high(s, c0, j):
                slot = j % R_RING
                a = a_tile(j % A_RING)
                act.wait_ge(a_loaded[j % A_RING], ph2_loaded(s, c0, j))
                act.wait_ge(s_used, PH1 + ph2_before(s, c0, j) - R_RING + 1)
                if j % 2:
                    act.activation(tile(square_ring, slot), a, ACT.Square)
                act.activation(tile(high_ring, slot), a, ACT.Square).then_inc(high_ready, 1)

            def pair(s, c0):
                for j in range(2 * PH2_N[s]):
                    par, k = divmod(j, PH2_N[s])
                    c = c0 + par
                    high(s, c0, j)
                    if k == 3 and not (isinstance(c, int) and c == 0):
                        store_out(c - 1, 1 - par)
                        if not (isinstance(c, int) and (c == NC - 1 or c == 1)):
                            load_acc(c + 1, 1 - par, c)
                    if isinstance(c, int) and c == 0:
                        if k == 4:
                            row_rstd(2 * NC - 1)
                        if k == PH2_N[0] - 1:
                            act.wait_ge(normed, 2 * NC)
                            load_acc(0, 0, None)
                            load_acc(1, 1, None)
                    if isinstance(c, int) and c == 1 and k == 5:
                        load_acc(2, 0, 1)

            phase2_pairs(act, pair, last_apart=True)
            store_out(NC - 1, 1)
            for par in range(2):
                act.wait_ge(out_stored[par], 16 * (NC // 2))

        @block.gpsimd
        def _(pool):
            pool.wait_ge(strip_zeroed, 1)
            eye = eye_strip[:, (GROUP - 1) * P:GROUP * P]
            pool.affine_select(out=eye, in_=eye, compare_op=ALU.not_equal, fill=1.0, base=0,
                               pattern=[[-1, P]], channel_multiplier=1).then_inc(strip_ready, 1)

            def square_deviation(n, b, cb, apart):
                pool.wait_ge(centred, n + 1)
                if not (isinstance(n, int) and n < 2):
                    pool.wait_ge(var_done, n - 1 if apart else n)
                pool.tensor_tensor(square_buf[b][:, :], centred_buf[cb][:, :], centred_buf[cb][:, :],
                                   ALU.mult).then_inc(dev_squared, 1)

            def relu(n):
                if n >= 2:
                    pool.wait_ge(projected, n - 1)
                pool.tensor_scalar(normed_buf[n % 2][:, :], centred_buf[n % 3][:, :], 0.0, None,
                                   ALU.max).then_inc(normed, 1)

            for n in range(NC):
                square_deviation(n, n % 2, n % 3, True)
                relu(n)

            def square_adj(s, c, p):
                n, r = l2_before(s, c, p), L2_RANK[s][p]
                pool.wait_ge(a_loaded[p % A_RING], 16 * load_rounds(s, c, p))
                if not (isinstance(n, int) and n < Q_RING):
                    pool.wait_ge(q_used, n - Q_RING + 1)
                blocks = ITEMS[s][p][1]
                a = blocks_of(a_ring, p % A_RING, blocks)
                pool.tensor_tensor(blocks_of(q_ring, r % Q_RING, blocks), a, a,
                                   ALU.mult).then_inc(q_ready, 1)

            def chunk(s, c):
                for p, (J, _, i) in enumerate(ITEMS[s]):
                    if i == POOL_SQUARE:
                        square_deviation(c + NC - 1, 0, 0, False)
                    if i is None or J < GROUP * s:
                        square_adj(s, c, p)

            phase1_chunks(pool, chunk)

            def pair(s, c0):
                for j in range(0, 2 * PH2_N[s], 2):
                    pool.wait_ge(a_loaded[j % A_RING], ph2_loaded(s, c0, j))
                    pool.wait_ge(s_used, PH1 + ph2_before(s, c0, j) - R_RING + 1)
                    a = a_tile(j % A_RING)
                    pool.tensor_tensor(tile(square_ring, j % R_RING), a, a,
                                       ALU.mult).then_inc(pool_square, 1)
                    if isinstance(c0, int) and c0 == 0 and j == 2:
                        square_deviation(2 * NC - 1, 0, 0, False)

            phase2_pairs(pool, pair)


def kernel(x, adj, L0_gnn_W, L0_gnn_B, L0_gnn_mu, L0_gnn_sigma, L1_gnn_W):
    import numpy as np
    import concourse.bacc as bacc
    from concourse.bass_utils import run_bass_kernel_spmd

    tiles = np.asarray(adj).reshape(NC, CHUNK, NC, G, P).transpose(0, 2, 4, 3, 1)
    arrays = {
        "xT": np.ascontiguousarray(np.asarray(x).T),
        "adjT": np.ascontiguousarray(tiles).reshape(NC * NC, P, TILE),
        "W0": np.ascontiguousarray(L0_gnn_W),
        "B0": np.ascontiguousarray(L0_gnn_B),
        "mu": np.ascontiguousarray(L0_gnn_mu),
        "sigma": np.ascontiguousarray(L0_gnn_sigma),
        "W1T": np.ascontiguousarray(np.asarray(L1_gnn_W).T),
    }
    nc = bacc.Bacc("TRN2", target_bir_lowering=False, num_devices=1)
    args = [nc.dram_tensor(name, a.shape, mybir.dt.from_np(a.dtype), kind="ExternalInput").ap()
            for name, a in arrays.items()]
    outT = nc.dram_tensor("outT", (D, N), F32, kind="ExternalOutput").ap()
    gnn_program(nc, *args, outT)
    r = run_bass_kernel_spmd(nc, [arrays], core_ids=[0])
    return np.ascontiguousarray(r.results[0]["outT"].T)
```
